# Optimizing a Trainium2 kernel written in Bass

```python
import numpy as np
import jax
import jax.numpy as jnp

def _softmax(x, axis=-1):
    return jax.nn.softmax(x, axis=axis)

def _gelu(x):
    return jax.nn.gelu(x, approximate=True)

def _silu(x):
    return jax.nn.silu(x)

def _sigmoid(x):
    return jax.nn.sigmoid(x)

def _layernorm(x, axis=-1, eps=1e-05):
    m = jnp.mean(x, axis=axis, keepdims=True)
    v = jnp.var(x, axis=axis, keepdims=True)
    return (x - m) / jnp.sqrt(v + eps)

def _scatter_add(tgt, idx, src, axis=0):
    return tgt.at[idx].add(src)

def _segment_sum(src, seg, n):
    return jax.ops.segment_sum(src, seg, n)
kernel_name = 'mk_xattn_seq_d4_seqx_r8_14e508'

def setup_inputs(seed: int=0):
    np.random.seed(seed)
    _w = jnp.asarray

    def _rec_inputs():
        import jax
        import jax.numpy as jnp
        _rk = jax.random.key(seed)
        x = -0.0002928 + 1 * jax.random.normal(jax.random.fold_in(_rk, 1), (32, 64, 256), jnp.float32)
        _lenS = 64 - jax.random.randint(jax.random.fold_in(_rk, 7), (32,), 0, max(1, 64 // 4) + 1, jnp.int32)
        _lenS2 = 64 - jax.random.randint(jax.random.fold_in(_rk, 8), (32,), 0, max(1, 64 // 4) + 1, jnp.int32)
        _ctx_2048P = jax.random.normal(jax.random.fold_in(_rk, 11), (32, 16, 256), jnp.float32)
        _ctx_2048c = jax.random.dirichlet(jax.random.fold_in(_rk, 511), 0.3 * jnp.ones((16,), jnp.float32), (32, 64))
        _ctx_2048t = jnp.einsum('bsk,bkd->bsd', _ctx_2048c, _ctx_2048P)
        _ctx_2048t = _ctx_2048t * jax.lax.rsqrt(jnp.mean(jnp.square(_ctx_2048t)) + 1e-12) * 0.953939
        ctx_2048 = -1.39393e-06 + 0.999914 * (_ctx_2048t + 0.3 * jax.random.normal(jax.random.fold_in(_rk, 611), (32, 64, 256), jnp.float32))
        _validS = jnp.arange(64)[None, :] < _lenS[:, None]
        _validS2 = jnp.arange(64)[None, :] < _lenS2[:, None]
        _causal = jnp.tril(jnp.ones((64, 64), dtype=bool))
        mask_BxS2_bf1 = jnp.ones((32, 64), dtype=bool)
        mask_BxS2_ik0 = jnp.where(jnp.broadcast_to(_validS2[:, :], (32, 64)), 0, 1).astype(jnp.int32)
        mask_1x1xSxS2_fc1 = jnp.where(jnp.broadcast_to(_validS2[0:1, None, None, :], (1, 1, 64, 64)), 1.0, 0.0).astype(jnp.float32)
        mask_Bx1xSxS2_ff1 = jnp.where(jnp.ones((32, 1, 64, 64), dtype=bool), 1.0, 0.0).astype(jnp.float32)
        return (x, ctx_2048, mask_BxS2_bf1, mask_BxS2_ik0, mask_1x1xSxS2_fc1, mask_Bx1xSxS2_ff1)
    x, ctx_2048, mask_BxS2_bf1, mask_BxS2_ik0, mask_1x1xSxS2_fc1, mask_Bx1xSxS2_ff1 = _rec_inputs()

    def _L0_xattn_setup():
        import jax, jax.numpy as jnp
        import numpy as np
        N, C, S, S2, H, CTX = (4, 64, 256, 256, 8, 64)
        EPS = 1e-05
        key = jax.random.key(seed)
        ks = jax.random.split(key, 6)
        sd = lambda fan: 1.0 / np.sqrt(fan)
        return {'input': jax.random.normal(ks[0], (N, C, S), jnp.float32), 'context': jax.random.normal(ks[1], (N, CTX, S2), jnp.float32), 'gamma': jnp.ones((C,), jnp.float32), 'beta': jnp.zeros((C,), jnp.float32), 'Wq': jax.random.normal(ks[2], (C * H, C), jnp.float32) * sd(C), 'bq': jnp.zeros((C * H,), jnp.float32), 'Wkv': jax.random.normal(ks[3], (C * H * 2, CTX), jnp.float32) * sd(CTX), 'bkv': jnp.zeros((C * H * 2,), jnp.float32), 'Wo': jax.random.normal(ks[4], (C, C * H), jnp.float32) * sd(C * H), 'bo': jnp.zeros((C,), jnp.float32)}
    _L0_xattn_all = _L0_xattn_setup()
    _L0_xattn_in = {k: v for k, v in _L0_xattn_all.items() if k in ('gamma', 'beta', 'Wq', 'bq', 'Wkv', 'bkv', 'Wo', 'bo')}
    del _L0_xattn_all

    def _L1_xattn_setup():
        import jax, jax.numpy as jnp
        import numpy as np
        HIDDEN = 256
        HEADS = 16
        HEAD_DIM = HIDDEN // HEADS
        LN_EPS = 1e-05
        GATE_INIT = 0.5

        def _layer_norm(x, gamma, beta):
            mu = jnp.mean(x, axis=-1, keepdims=True)
            var = jnp.mean(jnp.square(x - mu), axis=-1, keepdims=True)
            return (x - mu) * jax.lax.rsqrt(var + LN_EPS) * gamma + beta
        key = jax.random.key(seed)
        ks = jax.random.split(key, 8)
        B, T_TEXT, T_AUDIO = (4, 256, 1500)
        s = 0.02
        return {'hidden_states': jax.random.normal(ks[0], (B, T_TEXT, HIDDEN), jnp.float32), 'audio_kv': jax.random.normal(ks[1], (B, T_AUDIO, HIDDEN), jnp.float32), 'audio_attention_mask': jnp.ones((B, T_AUDIO), dtype=bool), 'Wq': jax.random.normal(ks[2], (HIDDEN, HIDDEN), jnp.float32) * s, 'Wk': jax.random.normal(ks[3], (HIDDEN, HIDDEN), jnp.float32) * s, 'Wv': jax.random.normal(ks[4], (HIDDEN, HIDDEN), jnp.float32) * s, 'Wo': jax.random.normal(ks[5], (HIDDEN, HIDDEN), jnp.float32) * s, 'ln_gamma': jnp.ones((HIDDEN,), jnp.float32), 'ln_beta': jnp.zeros((HIDDEN,), jnp.float32), 'gate': jnp.array([GATE_INIT], jnp.float32)}
    _L1_xattn_all = _L1_xattn_setup()
    _L1_xattn_in = {k: v for k, v in _L1_xattn_all.items() if k in ('Wq', 'Wk', 'Wv', 'Wo', 'ln_gamma', 'ln_beta', 'gate')}
    del _L1_xattn_all

    def _L2_xattn_setup():
        import jax, jax.numpy as jnp
        import numpy as np
        B, P, K, H, NH = (4, 256, 32, 256, 16)
        DH = H // NH
        EPS = 1e-06

        def rmsnorm(x, w):
            var = jnp.mean(jnp.square(x), axis=-1, keepdims=True)
            return x * jax.lax.rsqrt(var + EPS) * w
        key = jax.random.key(seed)
        ks = jax.random.split(key, 12)
        s = 0.02
        return {'x': jax.random.normal(ks[0], (B, P, H), jnp.float32), 'latents': jax.random.normal(ks[1], (B, K, H), jnp.float32), 'attention_mask': jax.random.randint(ks[2], (B, P), 0, 2, jnp.int32), 'q_w': s * jax.random.normal(ks[3], (H, H), jnp.float32), 'q_b': jnp.zeros((H,), jnp.float32), 'kv_w': s * jax.random.normal(ks[4], (H, 2 * H), jnp.float32), 'kv_b': jnp.zeros((2 * H,), jnp.float32), 'out_w': s * jax.random.normal(ks[5], (H, H), jnp.float32), 'out_b': jnp.zeros((H,), jnp.float32), 'postnorm_w': jnp.ones((H,), jnp.float32), 'mlp_w1': s * jax.random.normal(ks[6], (H, 4 * H), jnp.float32), 'mlp_b1': jnp.zeros((4 * H,), jnp.float32), 'mlp_w2': s * jax.random.normal(ks[7], (4 * H, H), jnp.float32), 'mlp_b2': jnp.zeros((H,), jnp.float32)}
    _L2_xattn_all = _L2_xattn_setup()
    _L2_xattn_in = {k: v for k, v in _L2_xattn_all.items() if k in ('q_w', 'q_b', 'kv_w', 'kv_b', 'out_w', 'out_b', 'postnorm_w', 'mlp_w1', 'mlp_b1', 'mlp_w2', 'mlp_b2')}
    del _L2_xattn_all

    def _L3_xattn_setup():
        import jax, jax.numpy as jnp
        import numpy as np
        H = 256
        NH = 16
        HD = H // NH
        EPS = 1e-05

        def gelu(x):
            return 0.5 * x * (1.0 + jnp.tanh(0.7978845608028654 * x * (1.0 + 0.044715 * x * x)))

        def layernorm(x, scale, bias):
            m = jnp.mean(x, axis=-1, keepdims=True)
            v = jnp.mean(jnp.square(x - m), axis=-1, keepdims=True)
            return (x - m) * jax.lax.rsqrt(v + EPS) * scale + bias

        def split_heads(x):
            b, s, _ = x.shape
            return x.reshape(b, s, NH, HD).transpose(0, 2, 1, 3)

        def merge_heads(x):
            b, nh, s, hd = x.shape
            return x.transpose(0, 2, 1, 3).reshape(b, s, nh * hd)

        def attention(q, k, v, mask):
            scores = jnp.einsum('bhqd,bhkd->bhqk', q, k) / jnp.sqrt(jnp.float32(HD))
            scores = scores * mask - 10000.0 * (1.0 - mask)
            probs = jax.nn.softmax(scores, axis=-1)
            return jnp.einsum('bhqk,bhkd->bhqd', probs, v)
        key = jax.random.key(seed)
        ks = jax.random.split(key, 16)
        b, s, t = (2, 128, 128)
        w = lambda k, i, o: jax.random.normal(k, (i, o), jnp.float32) * 0.02
        inp = {'hidden_states': jax.random.normal(ks[0], (b, s, H), jnp.float32), 'encoder_states': jax.random.normal(ks[1], (b, t, H), jnp.float32), 'ltor_mask': jnp.tril(jnp.ones((1, 1, s, s), jnp.float32)), 'cross_mask': jnp.ones((b, 1, s, t), jnp.float32), 'ln1_s': jnp.ones((H,), jnp.float32), 'ln1_b': jnp.zeros((H,), jnp.float32), 'w_qkv': w(ks[2], H, 3 * H), 'b_qkv': jnp.zeros((3 * H,), jnp.float32), 'w_ao': w(ks[3], H, H), 'b_ao': jnp.zeros((H,), jnp.float32), 'ln2_s': jnp.ones((H,), jnp.float32), 'ln2_b': jnp.zeros((H,), jnp.float32), 'w_q': w(ks[4], H, H), 'b_q': jnp.zeros((H,), jnp.float32), 'w_kv': w(ks[5], H, 2 * H), 'b_kv': jnp.zeros((2 * H,), jnp.float32), 'w_co': w(ks[6], H, H), 'b_co': jnp.zeros((H,), jnp.float32), 'ln3_s': jnp.ones((H,), jnp.float32), 'ln3_b': jnp.zeros((H,), jnp.float32), 'w1': w(ks[7], H, 4 * H), 'b1': jnp.zeros((4 * H,), jnp.float32), 'w2': w(ks[8], 4 * H, H), 'b2': jnp.zeros((H,), jnp.float32)}
        return inp
    _L3_xattn_all = _L3_xattn_setup()
    _L3_xattn_in = {k: v for k, v in _L3_xattn_all.items() if k in ('ln1_s', 'ln1_b', 'w_qkv', 'b_qkv', 'w_ao', 'b_ao', 'ln2_s', 'ln2_b', 'w_q', 'b_q', 'w_kv', 'b_kv', 'w_co', 'b_co', 'ln3_s', 'ln3_b', 'w1', 'b1', 'w2', 'b2')}
    del _L3_xattn_all
    return {'x': x, 'ctx_2048': ctx_2048, 'mask_BxS2_bf1': mask_BxS2_bf1, 'mask_BxS2_ik0': mask_BxS2_ik0, 'mask_1x1xSxS2_fc1': mask_1x1xSxS2_fc1, 'mask_Bx1xSxS2_ff1': mask_Bx1xSxS2_ff1, 'L0_xattn_gamma': _L0_xattn_in['gamma'], 'L0_xattn_beta': _L0_xattn_in['beta'], 'L0_xattn_Wq': _L0_xattn_in['Wq'], 'L0_xattn_bq': _L0_xattn_in['bq'], 'L0_xattn_Wkv': _L0_xattn_in['Wkv'], 'L0_xattn_bkv': _L0_xattn_in['bkv'], 'L0_xattn_Wo': _L0_xattn_in['Wo'], 'L0_xattn_bo': _L0_xattn_in['bo'], 'L1_xattn_Wq': _L1_xattn_in['Wq'], 'L1_xattn_Wk': _L1_xattn_in['Wk'], 'L1_xattn_Wv': _L1_xattn_in['Wv'], 'L1_xattn_Wo': _L1_xattn_in['Wo'], 'L1_xattn_ln_gamma': _L1_xattn_in['ln_gamma'], 'L1_xattn_ln_beta': _L1_xattn_in['ln_beta'], 'L1_xattn_gate': _L1_xattn_in['gate'], 'L2_xattn_q_w': _L2_xattn_in['q_w'], 'L2_xattn_q_b': _L2_xattn_in['q_b'], 'L2_xattn_kv_w': _L2_xattn_in['kv_w'], 'L2_xattn_kv_b': _L2_xattn_in['kv_b'], 'L2_xattn_out_w': _L2_xattn_in['out_w'], 'L2_xattn_out_b': _L2_xattn_in['out_b'], 'L2_xattn_postnorm_w': _L2_xattn_in['postnorm_w'], 'L2_xattn_mlp_w1': _L2_xattn_in['mlp_w1'], 'L2_xattn_mlp_b1': _L2_xattn_in['mlp_b1'], 'L2_xattn_mlp_w2': _L2_xattn_in['mlp_w2'], 'L2_xattn_mlp_b2': _L2_xattn_in['mlp_b2'], 'L3_xattn_ln1_s': _L3_xattn_in['ln1_s'], 'L3_xattn_ln1_b': _L3_xattn_in['ln1_b'], 'L3_xattn_w_qkv': _L3_xattn_in['w_qkv'], 'L3_xattn_b_qkv': _L3_xattn_in['b_qkv'], 'L3_xattn_w_ao': _L3_xattn_in['w_ao'], 'L3_xattn_b_ao': _L3_xattn_in['b_ao'], 'L3_xattn_ln2_s': _L3_xattn_in['ln2_s'], 'L3_xattn_ln2_b': _L3_xattn_in['ln2_b'], 'L3_xattn_w_q': _L3_xattn_in['w_q'], 'L3_xattn_b_q': _L3_xattn_in['b_q'], 'L3_xattn_w_kv': _L3_xattn_in['w_kv'], 'L3_xattn_b_kv': _L3_xattn_in['b_kv'], 'L3_xattn_w_co': _L3_xattn_in['w_co'], 'L3_xattn_b_co': _L3_xattn_in['b_co'], 'L3_xattn_ln3_s': _L3_xattn_in['ln3_s'], 'L3_xattn_ln3_b': _L3_xattn_in['ln3_b'], 'L3_xattn_w1': _L3_xattn_in['w1'], 'L3_xattn_b1': _L3_xattn_in['b1'], 'L3_xattn_w2': _L3_xattn_in['w2'], 'L3_xattn_b2': _L3_xattn_in['b2']}

def reference(x, ctx_2048, mask_BxS2_bf1, mask_BxS2_ik0, mask_1x1xSxS2_fc1, mask_Bx1xSxS2_ff1, L0_xattn_gamma, L0_xattn_beta, L0_xattn_Wq, L0_xattn_bq, L0_xattn_Wkv, L0_xattn_bkv, L0_xattn_Wo, L0_xattn_bo, L1_xattn_Wq, L1_xattn_Wk, L1_xattn_Wv, L1_xattn_Wo, L1_xattn_ln_gamma, L1_xattn_ln_beta, L1_xattn_gate, L2_xattn_q_w, L2_xattn_q_b, L2_xattn_kv_w, L2_xattn_kv_b, L2_xattn_out_w, L2_xattn_out_b, L2_xattn_postnorm_w, L2_xattn_mlp_w1, L2_xattn_mlp_b1, L2_xattn_mlp_w2, L2_xattn_mlp_b2, L3_xattn_ln1_s, L3_xattn_ln1_b, L3_xattn_w_qkv, L3_xattn_b_qkv, L3_xattn_w_ao, L3_xattn_b_ao, L3_xattn_ln2_s, L3_xattn_ln2_b, L3_xattn_w_q, L3_xattn_b_q, L3_xattn_w_kv, L3_xattn_b_kv, L3_xattn_w_co, L3_xattn_b_co, L3_xattn_ln3_s, L3_xattn_ln3_b, L3_xattn_w1, L3_xattn_b1, L3_xattn_w2, L3_xattn_b2):
    import jax
    import jax.numpy as jnp

    def _L0_xattn_ref(input, context, gamma, beta, Wq, bq, Wkv, bkv, Wo, bo):
        import jax, jax.numpy as jnp
        import numpy as np
        N, C, S, S2, H, CTX = (4, 64, 256, 256, 8, 64)
        EPS = 1e-05
        n, c, s = input.shape
        h = H
        mu = jnp.mean(input, axis=(1, 2), keepdims=True)
        var = jnp.var(input, axis=(1, 2), keepdims=True)
        xn = (input - mu) * jax.lax.rsqrt(var + EPS)
        xn = xn * gamma[None, :, None] + beta[None, :, None]
        q = jnp.einsum('oc,ncs->nos', Wq, xn) + bq[None, :, None]
        kv = jnp.einsum('od,nds->nos', Wkv, context) + bkv[None, :, None]
        q = q.reshape(n, h, c, s).transpose(0, 1, 3, 2)
        kv = kv.reshape(n, 2 * h, c, -1).transpose(0, 1, 3, 2)
        k, v = (kv[:, :h], kv[:, h:])
        scale = c ** (-0.25)
        att = jax.nn.softmax(jnp.einsum('nhqc,nhkc->nhqk', q * scale, k * scale), axis=-1)
        y = jnp.einsum('nhqk,nhkc->nhqc', att, v)
        y = y.transpose(0, 1, 3, 2).reshape(n, h * c, s)
        out = jnp.einsum('co,nos->ncs', Wo, y) + bo[None, :, None]
        return input + out

    def _L1_xattn_ref(hidden_states, audio_kv, audio_attention_mask, Wq, Wk, Wv, Wo, ln_gamma, ln_beta, gate):
        import jax, jax.numpy as jnp
        import numpy as np
        HIDDEN = 256
        HEADS = 16
        HEAD_DIM = HIDDEN // HEADS
        LN_EPS = 1e-05
        GATE_INIT = 0.5

        def _layer_norm(x, gamma, beta):
            mu = jnp.mean(x, axis=-1, keepdims=True)
            var = jnp.mean(jnp.square(x - mu), axis=-1, keepdims=True)
            return (x - mu) * jax.lax.rsqrt(var + LN_EPS) * gamma + beta
        B, Tt, D = hidden_states.shape
        Ta = audio_kv.shape[1]
        scale = HEAD_DIM ** (-0.5)
        a = _layer_norm(audio_kv, ln_gamma, ln_beta)
        Q = (hidden_states @ Wq.T).reshape(B, Tt, HEADS, HEAD_DIM).transpose(0, 2, 1, 3)
        K = (a @ Wk.T).reshape(B, Ta, HEADS, HEAD_DIM).transpose(0, 2, 1, 3)
        V = (a @ Wv.T).reshape(B, Ta, HEADS, HEAD_DIM).transpose(0, 2, 1, 3)
        scores = jnp.einsum('bhtd,bhsd->bhts', Q, K) * scale
        mask = audio_attention_mask[:, None, None, :]
        scores = jnp.where(mask, scores, jnp.float32(-jnp.inf))
        attn = jax.nn.softmax(scores, axis=-1)
        out = jnp.einsum('bhts,bhsd->bhtd', attn, V)
        out = out.transpose(0, 2, 1, 3).reshape(B, Tt, D)
        out = out @ Wo.T
        return hidden_states + jnp.tanh(gate) * out

    def _L2_xattn_ref(x, latents, attention_mask, q_w, q_b, kv_w, kv_b, out_w, out_b, postnorm_w, mlp_w1, mlp_b1, mlp_w2, mlp_b2):
        import jax, jax.numpy as jnp
        import numpy as np
        B, P, K, H, NH = (4, 256, 32, 256, 16)
        DH = H // NH
        EPS = 1e-06

        def rmsnorm(x, w):
            var = jnp.mean(jnp.square(x), axis=-1, keepdims=True)
            return x * jax.lax.rsqrt(var + EPS) * w
        b, p, _ = x.shape
        k_len = latents.shape[1]
        residual = latents
        h = jnp.concatenate([x, latents], axis=1)
        q = (latents @ q_w + q_b).reshape(b, k_len, NH, DH)
        kv = (h @ kv_w + kv_b).reshape(b, p + k_len, NH, DH, 2)
        kmat, v = (kv[..., 0], kv[..., 1])
        attn = jnp.einsum('bkhd,bnhd->bhkn', q, kmat) / DH
        full_mask = jnp.concatenate([attention_mask.astype(bool), jnp.ones((b, k_len), bool)], axis=-1)
        attn = jnp.where(full_mask[:, None, None, :], attn, -jnp.inf)
        attn = jax.nn.softmax(attn.astype(jnp.float32), axis=-1).astype(q.dtype)
        attn_out = jnp.einsum('bhkn,bnhd->bkhd', attn, v).reshape(b, k_len, H)
        attn_out = attn_out @ out_w + out_b + residual
        out = rmsnorm(attn_out, postnorm_w)
        out = jax.nn.gelu(out @ mlp_w1 + mlp_b1) @ mlp_w2 + mlp_b2
        return out + residual

    def _L3_xattn_ref(hidden_states, encoder_states, ltor_mask, cross_mask, ln1_s, ln1_b, w_qkv, b_qkv, w_ao, b_ao, ln2_s, ln2_b, w_q, b_q, w_kv, b_kv, w_co, b_co, ln3_s, ln3_b, w1, b1, w2, b2):
        import jax, jax.numpy as jnp
        import numpy as np
        H = 256
        NH = 16
        HD = H // NH
        EPS = 1e-05

        def gelu(x):
            return 0.5 * x * (1.0 + jnp.tanh(0.7978845608028654 * x * (1.0 + 0.044715 * x * x)))

        def layernorm(x, scale, bias):
            m = jnp.mean(x, axis=-1, keepdims=True)
            v = jnp.mean(jnp.square(x - m), axis=-1, keepdims=True)
            return (x - m) * jax.lax.rsqrt(v + EPS) * scale + bias

        def split_heads(x):
            b, s, _ = x.shape
            return x.reshape(b, s, NH, HD).transpose(0, 2, 1, 3)

        def merge_heads(x):
            b, nh, s, hd = x.shape
            return x.transpose(0, 2, 1, 3).reshape(b, s, nh * hd)

        def attention(q, k, v, mask):
            scores = jnp.einsum('bhqd,bhkd->bhqk', q, k) / jnp.sqrt(jnp.float32(HD))
            scores = scores * mask - 10000.0 * (1.0 - mask)
            probs = jax.nn.softmax(scores, axis=-1)
            return jnp.einsum('bhqk,bhkd->bhqd', probs, v)
        ln_out = layernorm(hidden_states, ln1_s, ln1_b)
        qkv = ln_out @ w_qkv + b_qkv
        q, k, v = jnp.split(qkv, 3, axis=-1)
        ctx = merge_heads(attention(split_heads(q), split_heads(k), split_heads(v), ltor_mask))
        attn_out = ctx @ w_ao + b_ao
        x = hidden_states + attn_out
        ln_out = layernorm(x, ln2_s, ln2_b)
        q = ln_out @ w_q + b_q
        kv = encoder_states @ w_kv + b_kv
        k, v = jnp.split(kv, 2, axis=-1)
        ctx = merge_heads(attention(split_heads(q), split_heads(k), split_heads(v), cross_mask))
        cross_out = ctx @ w_co + b_co
        x = x + cross_out
        ln_out = layernorm(x, ln3_s, ln3_b)
        mlp_out = gelu(ln_out @ w1 + b1) @ w2 + b2
        return x + mlp_out
    x = _L0_xattn_ref(x, ctx_2048, L0_xattn_gamma, L0_xattn_beta, L0_xattn_Wq, L0_xattn_bq, L0_xattn_Wkv, L0_xattn_bkv, L0_xattn_Wo, L0_xattn_bo)
    x = _L1_xattn_ref(x, ctx_2048, mask_BxS2_bf1, L1_xattn_Wq, L1_xattn_Wk, L1_xattn_Wv, L1_xattn_Wo, L1_xattn_ln_gamma, L1_xattn_ln_beta, L1_xattn_gate)
    x = _L2_xattn_ref(ctx_2048, x, mask_BxS2_ik0, L2_xattn_q_w, L2_xattn_q_b, L2_xattn_kv_w, L2_xattn_kv_b, L2_xattn_out_w, L2_xattn_out_b, L2_xattn_postnorm_w, L2_xattn_mlp_w1, L2_xattn_mlp_b1, L2_xattn_mlp_w2, L2_xattn_mlp_b2)
    x = _L3_xattn_ref(x, ctx_2048, mask_1x1xSxS2_fc1, mask_Bx1xSxS2_ff1, L3_xattn_ln1_s, L3_xattn_ln1_b, L3_xattn_w_qkv, L3_xattn_b_qkv, L3_xattn_w_ao, L3_xattn_b_ao, L3_xattn_ln2_s, L3_xattn_ln2_b, L3_xattn_w_q, L3_xattn_b_q, L3_xattn_w_kv, L3_xattn_b_kv, L3_xattn_w_co, L3_xattn_b_co, L3_xattn_ln3_s, L3_xattn_ln3_b, L3_xattn_w1, L3_xattn_b1, L3_xattn_w2, L3_xattn_b2)
    return x

_drawn_inputs = setup_inputs


def setup_inputs(seed=0):
    import zlib

    import numpy as np

    out = dict(_drawn_inputs(seed))
    spreads = {'L0_xattn_gamma': (1.0, 0.2),
     'L0_xattn_beta': (0.0, 0.267),
     'L0_xattn_bq': (0.0, 0.1),
     'L0_xattn_bkv': (0.0, 0.1),
     'L0_xattn_bo': (0.0, 0.1),
     'L1_xattn_ln_gamma': (1.0, 0.6),
     'L1_xattn_ln_beta': (0.0, 0.8),
     'L2_xattn_q_b': (0.0, 0.8),
     'L2_xattn_kv_b': (0.0, 0.8),
     'L2_xattn_out_b': (0.0, 0.728),
     'L2_xattn_postnorm_w': (1.0, 0.6),
     'L2_xattn_mlp_b1': (0.0, 0.1),
     'L2_xattn_mlp_b2': (0.0, 0.1),
     'L3_xattn_ln1_s': (1.0, 0.6),
     'L3_xattn_ln1_b': (0.0, 0.791),
     'L3_xattn_b_qkv': (0.0, 0.278),
     'L3_xattn_b_ao': (0.0, 0.1),
     'L3_xattn_ln2_s': (1.0, 0.6),
     'L3_xattn_ln2_b': (0.0, 0.8),
     'L3_xattn_b_q': (0.0, 0.8),
     'L3_xattn_b_kv': (0.0, 0.284),
     'L3_xattn_b_co': (0.0, 0.1),
     'L3_xattn_ln3_s': (1.0, 0.6),
     'L3_xattn_ln3_b': (0.0, 0.735),
     'L3_xattn_b1': (0.0, 0.1),
     'L3_xattn_b2': (0.0, 0.1)}
    factors = {'L1_xattn_Wq': 8.0,
     'L1_xattn_Wk': 8.0,
     'L2_xattn_q_w': 8.0,
     'L2_xattn_kv_w': 8.0,
     'L2_xattn_out_w': 8.0,
     'L3_xattn_w_qkv': 2.822,
     'L3_xattn_w_q': 8.0}
    for name, (base, spread) in spreads.items():
        noise = np.random.default_rng([zlib.crc32(name.encode()), seed]).standard_normal(out[name].shape)
        drawn = base * np.exp(spread * noise) if base else spread * noise
        out[name] = jnp.asarray(drawn.astype(out[name].dtype))
    for name, factor in factors.items():
        out[name] = (out[name] * factor).astype(out[name].dtype)
    return out
```

```python
from contextlib import ExitStack

import numpy as np
import concourse.bass as bass
from concourse import mybir

F32 = mybir.dt.float32
F32R = mybir.dt.float32r
U8 = mybir.dt.uint8
I32 = mybir.dt.int32
ALU = mybir.AluOpType
ACT = mybir.ActivationFunctionType
AX = mybir.AxisListType

P = 128
NSEQ, S, D = 32, 64, 256
PAIRS = NSEQ // 2
KT = D // P
H0 = 8
HEADS, HD = 16, 16
HB = HEADS // KT
HID = 4 * D
MT = HID // P
NEG = -1.0e30

COLS = {}
for _name, _n in (("l0_gamma", 1), ("l0_beta", 1), ("l0_bo", 1), ("l0_bq", H0), ("l0_bk", H0),
                  ("l1_g", KT), ("l1_b", KT),
                  ("l2_bq", KT), ("l2_bk", KT), ("l2_bv", KT), ("l2_post", KT), ("l2_b1", MT),
                  ("l3_g1", KT), ("l3_b1n", KT), ("l3_bqkv", 3 * KT), ("l3_g2", KT), ("l3_b2n", KT),
                  ("l3_bq", KT), ("l3_bk", KT), ("l3_bv", KT), ("l3_g3", KT), ("l3_b3n", KT), ("l3_b1", MT)):
    COLS[_name] = (sum(n for _, n in COLS.values()), _n)
NCOLS = sum(n for _, n in COLS.values())
ROWS = ["l2_bo", "l2_b2", "l3_bao", "l3_bco", "l3_b2"]

WB = {"q0": (KT, D), "k0": (KT, D), "v0": (KT, D), "o0": (KT, D),
      "q1": (KT, D), "k1": (KT, D), "v1": (KT, D), "o1": (KT, D), "w1": (KT, HID), "w2": (MT, D)}
WC = dict(WB)
WCOLS = sum(a * b for a, b in WB.values())

def attention_fills(a, blocks):
    return ([(a, "s", f, c) for f in range(KT) for c in range(blocks)]
            + [x for f in range(KT) for x in [(a, "t", f, c) for c in range(blocks)] + [(a, "o", f)]]
            + [(a, "p")])


FILLS_B = (["xT", "nT0"] + [(0, "q"), (0, "k", 0), (0, "v", 0)] + attention_fills(0, 1) + ["x2T"]
           + [(1, "q"), (1, "k", 0), (1, "k", 1), (1, "v", 0), (1, "v", 1)] + attention_fills(1, 2)
           + ["nT1", "h0", "h1", "y"])
FILLS_C = (["xT", "nT0"] + [(0, "q"), (0, "k", 0), (0, "v", 0)] + attention_fills(0, 1)
           + ["nT1"] + [(1, "q"), (1, "k", 0), (1, "v", 0)] + attention_fills(1, 1)
           + ["nT2", "h0", "h1", "y"])


ORDER = {
    "pool": "bbacacbbccbbcaacbccababbbcccaacccaacbbccaaccaabbaaaa",
    "pe": "bcabababaaacbcbacbcacacbababbbaababaacbabcacbcaabcabaaabacbcccaabacaaacaaaaaabbacabccaabcacbaaacbacbccbaabaaacaabaabaabaaaaa",
    "act": "abcbbaaacabaabcababbcbaabaabcacacacbcaabaaacbcaabaaacaabcbaacabccaabcbacabaccbaabaaaabaaaa",
    "dve": "babbaaacaccbacbbcbabbabcacaacaabcaccbaaaababaaccabaacababcacbababcaaacaacbabcacacaaaaaacccaaaacbbabcabaaaacaabaaabaaaaa",
}
LENGTH = {"a": 47.0, "b": 41.0, "c": 43.0}


def weave(engine, programs):
    if engine in ORDER:
        for program in programs.values():
            next(program)
        for stage in ORDER[engine]:
            if stage in programs:
                next(programs[stage], None)
        return
    waiting = []
    for name, program in programs.items():
        waiting.append([next(program) / LENGTH[name], name, program])
    while waiting:
        first = min(waiting, key=lambda w: (w[0], w[1]))
        step = next(first[2], None)
        if step is None:
            waiting.remove(first)
        else:
            first[0] = max(first[0], step / LENGTH[first[1]])


class Stage:
    pass


def build(nc, dram, out):
    ctx = ExitStack()
    with ctx:
        sb = lambda name, shape, dt=F32: ctx.enter_context(nc.sbuf_tensor(name, shape, dt))
        bank = lambda name: ctx.enter_context(nc.psum_tensor(name, [P, 512], F32))
        sems = []

        def sem(name):
            sems.append(ctx.enter_context(nc.semaphore(name)))
            return sems[-1]

        ident = sb("ident", [P, P])
        mean_of_all = sb("mean_of_all", [P, P])
        minus_half = sb("minus_half", [P, 2])
        head_mask = sb("head_mask", [P, HB])
        cols = sb("cols", [P, NCOLS])
        col = lambda name: cols[:, COLS[name][0]:COLS[name][0] + COLS[name][1]]
        gate = sb("gate", [P, 1])
        tanh_gate = sb("tanh_gate", [P, 1])
        bv_raw = sb("bv_raw", [S, H0])
        wq_split = sb("wq_split", [P, H0, P], F32R)
        wk_split = sb("wk_split", [P, H0, P], F32R)
        wvo_hi = sb("wvo_hi", [P, H0 * S], F32R)
        wvo_lo = sb("wvo_lo", [P, H0 * S], F32R)
        out_bias0 = sb("out_bias0", [P, 1])
        wb = sb("wb", [P, WCOLS])
        wc = sb("wc", [P, WCOLS])

        def weights(tile, table):
            got, at = {}, 0
            for name, (a, b) in table.items():
                got[name] = tile[:, at:at + a * b].rearrange("p (a b) -> p a b", a=a)
                at += a * b
            return got

        WBt, WCt = weights(wb, WB), weights(wc, WC)
        fold = sb("fold", [P, 20])
        FOLD = {"bk1": (0, KT), "bv1": (2, KT), "q3": (4, KT), "k3": (6, KT), "v3": (8, KT), "q4": (10, KT), "b1": (12, MT)}
        fcol = lambda name: fold[:, FOLD[name][0]:FOLD[name][0] + FOLD[name][1]]
        row_bias = sb("row_bias", [P, 6, D])
        self_mul = sb("self_mul", [P, S])
        self_add = sb("self_add", [P, S])
        self_raw = sb("self_raw", [P, S])

        x_dup = sb("x_dup", [P, 2, D])
        c_dup = sb("c_dup", [P, 2, D])
        x_nat = sb("x_nat", [P, D])
        res_a = sb("res_a", [P, D])
        stats_a = sb("stats_a", [P, 2, 6])
        mv_a = sb("mv_a", [P, 2, 2])
        small_a = sb("small_a", [P, 8, 2])
        xn_a = sb("xn_a", [P, 2, D])
        x_hi = sb("x_hi", [P, 2, D], F32R)
        x_lo = sb("x_lo", [P, 2, D], F32R)
        c_hi = sb("c_hi", [P, 2, D], F32R)
        c_lo = sb("c_lo", [P, 2, D], F32R)
        c_split = sb("c_split", [P, 2, D], F32R)
        q_split = sb("q_split", [P, 2, D], F32R)
        k_hi = sb("k_hi", [P, 2, D], F32R)
        k_lo = sb("k_lo", [P, 2, D], F32R)
        v_a = sb("v_a", [P, 2, KT, H0 * S])
        p_a = sb("p_a", [P, 2, KT, D])
        pt_a = sb("pt_a", [P, 2, KT, D])
        max_a = sb("max_a", [P, 2, KT])
        nmax_a = sb("nmax_a", [P, 2, KT])
        sum_a = sb("sum_a", [P, 2, KT])
        rec_a = sb("rec_a", [P, 2, KT])
        x1 = sb("x1", [P, D])

        scores_bank = [bank("scores0"), bank("scores1")]
        transposed_bank = bank("transposed")
        project_bank = bank("project")
        attended_bank = bank("attended")

        A = {n: sem("a_" + n) for n in (
            "stats", "mv", "mean_ps", "mean", "dev", "sq", "var", "var_ps", "eps", "rstd", "scale", "shift", "bias",
            "norm", "xhi", "xlo", "chi", "clo", "csplit", "v_ps", "v_sb", "q_ps", "q_hi", "q_lo", "k_ps", "k_hi",
            "k_lo", "scores", "max", "nmax", "exp", "rec", "prob", "trans", "pt0", "pt1", "att", "res", "x1")}

        def stage(name, banks, fills, blocks, W):
            T = Stage()
            T.banks, T.fills, T.W = banks, {f: n for n, f in enumerate(fills)}, W
            t = lambda n, shape, dt=F32: sb(f"{name}_{n}", shape, dt)
            T.c = t("c", [P, D])
            T.stats, T.mv, T.eps, T.msq, T.rstd = t("stats", [P, 6]), t("mv", [P, 2]), t("eps", [P, 1]), t("msq", [P, 1]), t("rstd", [P, 1])
            T.xn = t("xn", [P, D])
            T.xnT = t("xnT", [P, KT, P])
            T.xT = t("xT", [P, blocks * KT, P])
            T.qT = t("qT", [P, KT, P])
            T.kT = t("kT", [P, blocks, KT, P])
            T.kblk = t("kblk", [P, KT, blocks, 2, HB, S])
            T.v = t("v", [P, blocks, 2, HEADS // 2, 2, HD])
            T.p = t("p", [P, KT, HB * blocks * S])
            T.pt = t("pt", [P, KT, blocks, HB // 2, P])
            T.max, T.sum, T.rec = t("max", [P, KT, HB]), t("sum", [P, KT, HB]), t("rec", [P, KT, HB])
            T.yT = t("yT", [P, KT, P])
            T.res = t("res", [P, D])
            T.mid = t("mid", [P, 2, D])
            T.hid = T.pt[:, :, :, :, :].rearrange("p f c g q -> p (f c g) q")[:, 0:MT, :]
            T.s = {n: sem(f"{name}_{n}") for n in (
                "stats", "mv", "eps", "msq", "rstd", "xn", "mask", "kblk", "madd", "max", "sub", "exp", "sum", "rec",
                "prob", "res", "hid")}
            T.full = [sem(f"{name}_full{i}") for i in range(len(banks))]
            T.free = [sem(f"{name}_free{i}") for i in range(len(banks))]
            return T

        B = stage("b", [bank("b_bank0")], FILLS_B, 2, WBt)
        B.x2T = sb("b_x2T", [P, KT, P])
        C = stage("c", [bank("c_bank0"), bank("c_bank1")], FILLS_C, 1, WCt)
        def views(scratch, table):
            got, at = [], 0
            for parts, a, b in table:
                got.append(scratch[0:parts, at:at + a * b].rearrange("p (a b) -> p a b", a=a))
                at += a * b
            return got

        rows, wq_raw, wk_raw, wo_raw = views(B.kblk[:, :, :, :, :, :].rearrange("p f c b h k -> p (f c b h k)"),
                                             ((P, len(ROWS), D), (P, H0, P), (P, H0, P), (S, H0, S)))
        wv_raw, spread = views(B.p[:, :, :].rearrange("p f k -> p (f k)"), ((S, H0, P), (P, 4 * KT, P)))
        spread = spread.rearrange("p (n k) q -> p n k q", k=KT)
        x3 = sb("x3", [P, D])
        y_out = sb("y_out", [P, D])
        m1_raw = sb("m1_raw", [P, S], U8)
        m2_raw = sb("m2_raw", [P, S], I32)
        m1 = sb("m1", [P, S])
        m2 = sb("m2", [P, S])
        m4_raw = sb("m4_raw", [P, S])
        m4_mul = sb("m4_mul", [P, S])
        m4_add = sb("m4_add", [P, S])
        loaded = sem("loaded")
        stored = sem("stored")
        setup = {n: sem("setup_" + n) for n in ("consts", "zeros", "raw", "fold_ps", "fold", "mid_ps", "mid", "step", "tanh", "scaled", "spread", "row_ps", "row")}
        clear = range(min(s.num for s in sems), max(s.num for s in sems) + 1)
        assert len(clear) == len(sems)

        def fill_bank(T, eng, name):
            n = T.fills[name]
            i, k = n % len(T.banks), n // len(T.banks)
            if k:
                eng.wait_ge(T.free[i], k)
            return T.banks[i]

        def filled(T, ins, name):
            ins.then_inc(T.full[T.fills[name] % len(T.banks)], 1)

        def wait_fill(T, eng, name):
            n = T.fills[name]
            eng.wait_ge(T.full[n % len(T.banks)], n // len(T.banks) + 1)
            return T.banks[n % len(T.banks)]

        def release(T, ins, name):
            ins.then_inc(T.free[T.fills[name] % len(T.banks)], 1)

        def bc(ap, axis, n):
            ap = ap.unsqueeze(axis)
            shape = list(ap.shape)
            shape[axis] = n
            return ap.to_broadcast(shape)

        mm = nc.tensor.matmul

        def load_a(sp, i):
            for dup in range(2):
                sp.dma_start(x_dup[dup * S:(dup + 1) * S, :, :], dram["x"][pair(i)].rearrange("n c s -> c n s")).then_inc(loaded, 16)
                sp.dma_start(c_dup[dup * S:(dup + 1) * S, :, :], dram["ctx"][pair(i)].rearrange("n c s -> c n s")).then_inc(loaded, 16)
            sp.dma_start(x_nat[:, :], dram["x"][pair(i)].rearrange("n c s -> (n c) s")).then_inc(loaded, 16)
            return 5 * 16

        def pair(i):
            return bass.ds(2 * i, 2)

        with nc.Block() as block:

            @block.sync
            def _(sp):
                n = 0
                for dst, src in ((cols[:, :], dram["cols"]), (rows[:, :, :], dram["rows"].partition_broadcast(P)),
                                 (gate[:, :], dram["gate"].partition_broadcast(P)),
                                 (wq_raw[:, :, :], dram["wq0"]), (wk_raw[:, :, :], dram["wk0"]),
                                 (wv_raw[:, :, :], dram["wv0"]), (wo_raw[:, :, :], dram["wo0"]), (bv_raw[:, :], dram["bv0"]),
                                 (self_raw[0:S, :], dram["self_mask"]), (self_raw[S:P, :], dram["self_mask"]),
                                 (wb[:, :], dram["wb"]), (wc[:, :], dram["wc"])):
                    sp.dma_start(dst, src).then_inc(loaded, 16)
                    n += 16
                n += load_a(sp, 0)
                sp.wait_ge(loaded, n)
                sp.sem_inc(setup["raw"], 1)

            @block.gpsimd
            def _(pool):
                pool.memset(ident[:, :], 0.0).then_inc(setup["zeros"], 1)
                pool.memset(head_mask[:, :], 1.0).then_inc(setup["zeros"], 1)
                pool.memset(mean_of_all[:, :], 1.0 / P).then_inc(setup["consts"], 1)
                pool.memset(minus_half[:, :], -0.5).then_inc(setup["consts"], 1)
                pool.memset(B.v[:, :, :, :, :, :], 0.0).then_inc(setup["consts"], 1)
                pool.memset(C.v[:, :, :, :, :, :], 0.0).then_inc(setup["consts"], 1)
                pool.wait_ge(setup["zeros"], 2)
                pool.affine_select(out=ident[:, :], in_=ident[:, :], compare_op=ALU.not_equal, fill=1.0,
                                   base=0, pattern=[[-1, P]], channel_multiplier=1).then_inc(setup["consts"], 1)
                pool.affine_select(out=head_mask[:, :], in_=head_mask[:, :], compare_op=ALU.is_ge, fill=0.0,
                                   base=0, pattern=[[-HD, HB]], channel_multiplier=1).then_inc(setup["zeros"], 1)
                pool.wait_ge(setup["zeros"], 3)
                pool.affine_select(out=head_mask[:, :], in_=head_mask[:, :], compare_op=ALU.is_ge, fill=0.0,
                                   base=HD - 1, pattern=[[HD, HB]], channel_multiplier=-1).then_inc(setup["consts"], 1)

            @block.tensor
            def _(pe):
                pe.wait_ge(setup["raw"], 1)
                for h in range(H0):
                    last = mm(scores_bank[0][:, h * S:(h + 1) * S], wv_raw[:, h, :], wo_raw[:, h, :], start=True, stop=True)
                last.then_inc(setup["mid_ps"], 1)
                for h in range(H0):
                    for half in range(2):
                        last = mm(scores_bank[1][half * S:(half + 1) * S, 0:1], wo_raw[:, h, :], bv_raw[:, h:h + 1],
                                  start=h == 0, stop=h == H0 - 1)
                last.then_inc(setup["mid_ps"], 1)
                at = 0
                for W, name, beta, n in ((WBt, "k0", "l1_b", KT), (WBt, "v0", "l1_b", KT), (WCt, "q0", "l3_b1n", KT),
                                         (WCt, "k0", "l3_b1n", KT), (WCt, "v0", "l3_b1n", KT), (WCt, "q1", "l3_b2n", KT),
                                         (WCt, "w1", "l3_b3n", MT)):
                    for m in range(n):
                        for k in range(KT):
                            last = mm(project_bank[:, at:at + 1], W[name][:, k, m * P:(m + 1) * P], col(beta)[:, k:k + 1],
                                      start=k == 0, stop=k == KT - 1)
                        at += 1
                last.then_inc(setup["fold_ps"], 1)
                pe.wait_ge(setup["spread"], 4)
                pe.wait_ge(setup["scaled"], 9)
                for n, (W, name) in enumerate(((WBt, "o0"), (WBt, "o1"), (WCt, "o0"), (WCt, "o1"))):
                    ps = (transposed_bank, attended_bank)[n % 2]
                    for k in range(KT):
                        last = mm(ps[:, (n // 2) * D:(n // 2 + 1) * D], spread[:, n, k, :], W[name][:, k, :],
                                  start=k == 0, stop=k == KT - 1)
                    last.then_inc(setup["row_ps"], 1)

            @block.scalar
            def _(act):
                act.wait_ge(setup["raw"], 1)
                nc.scalar.activation(tanh_gate[:, :], gate[:, :], ACT.Tanh).then_inc(setup["tanh"], 1)

            @block.vector
            def _(dve):
                dve.wait_ge(setup["raw"], 1)
                for n, (split, raw) in enumerate(((wq_split, wq_raw), (wk_split, wk_raw))):
                    dve.tensor_copy(split[:, :, :], raw[:, :, :]).then_inc(setup["step"], 1)
                    dve.wait_ge(setup["step"], n + 1)
                    dve.tensor_tensor(split[S:P, :, :], raw[S:P, :, :], split[S:P, :, :].bitcast(F32), ALU.subtract)
                dve.wait_ge(setup["mid_ps"], 2)
                dve.tensor_copy(wvo_hi[:, :], scores_bank[0][:, :]).then_inc(setup["step"], 1)
                dve.wait_ge(setup["step"], 3)
                dve.tensor_tensor(wvo_lo[:, :], scores_bank[0][:, :], wvo_hi[:, :].bitcast(F32), ALU.subtract)
                dve.tensor_tensor(out_bias0[:, :], scores_bank[1][:, 0:1], col("l0_bo"), ALU.add)
                dve.tensor_scalar(self_mul[:, :], self_raw[:, :], HD ** -0.5, None, ALU.mult)
                dve.tensor_scalar(self_add[:, :], self_raw[:, :], 10000.0, -10000.0, ALU.mult, ALU.add)
                dve.wait_ge(setup["fold_ps"], 1)
                for name, base in (("bk1", None), ("bv1", None), ("q3", "l3_bqkv"), ("q4", "l3_bq"), ("b1", "l3_b1")):
                    at = FOLD[name][0]
                    n = 3 * KT if name == "q3" else FOLD[name][1]
                    if base:
                        ins = dve.tensor_tensor(fold[:, at:at + n], project_bank[:, at:at + n], col(base), ALU.add)
                    else:
                        ins = dve.tensor_copy(fold[:, at:at + n], project_bank[:, at:at + n])
                    ins.then_inc(setup["fold"], 1)
                dve.wait_ge(setup["fold"], 5)
                for n, vec in enumerate((fcol("bv1"), col("l2_bv"), fcol("v3"), col("l3_bv"))):
                    dve.tensor_copy(spread[:, n, :, :], bc(vec, 2, P)).then_inc(setup["spread"], 1)
                dve.wait_ge(setup["tanh"], 1)
                for W, name, g in ((WBt, "k0", "l1_g"), (WBt, "v0", "l1_g"), (WBt, "w1", "l2_post"), (WCt, "q0", "l3_g1"),
                                   (WCt, "k0", "l3_g1"), (WCt, "v0", "l3_g1"), (WCt, "q1", "l3_g2"), (WCt, "w1", "l3_g3")):
                    for k in range(KT):
                        last = dve.tensor_scalar(W[name][:, k, :], W[name][:, k, :], col(g)[:, k:k + 1], None, ALU.mult)
                    last.then_inc(setup["scaled"], 1)
                dve.tensor_scalar(WBt["o0"], WBt["o0"], tanh_gate[:, :], None, ALU.mult).then_inc(setup["scaled"], 1)
                dve.wait_ge(setup["row_ps"], 4)
                for at, n, base in ((0, 0, None), (1, 1, "l2_bo"), (3, 2, "l3_bao"), (4, 3, "l3_bco")):
                    ps = (transposed_bank, attended_bank)[n % 2][:, (n // 2) * D:(n // 2 + 1) * D]
                    if base:
                        dve.tensor_tensor(row_bias[:, at, :], ps, rows[:, ROWS.index(base), :], ALU.add)
                    else:
                        dve.tensor_copy(row_bias[:, at, :], ps)
                dve.tensor_copy(row_bias[:, 2, :], rows[:, ROWS.index("l2_b2"), :])
                dve.tensor_copy(row_bias[:, 5, :], rows[:, ROWS.index("l3_b2"), :])

        def load_b(sp, i):
            sp.dma_start(B.c[:, :], dram["ctx"][pair(i)].rearrange("n c s -> (n c) s")).then_inc(loaded, 16)
            for b in range(2):
                sp.dma_start(m1_raw[b * S:(b + 1) * S, :], dram["mask1"][bass.ds(2 * i + b, 1), :].rearrange("o k -> (o k)").partition_broadcast(S)).then_inc(loaded, 16)
                sp.dma_start(m2_raw[b * S:(b + 1) * S, :], dram["mask2"][bass.ds(2 * i + b, 1), :].rearrange("o k -> (o k)").partition_broadcast(S)).then_inc(loaded, 16)
            return 5 * 16

        def load_c(sp, i):
            sp.dma_start(C.c[:, :], dram["ctx"][pair(i)].rearrange("n c s -> (n c) s")).then_inc(loaded, 16)
            sp.dma_start(m4_raw[:, :], dram["mask4"][pair(i)].rearrange("n q k -> (n q) k")).then_inc(loaded, 16)
            return 2 * 16

        nc.all_engine_barrier(sems_to_clear=clear)

        def head_step(h, k=0.0):
            return 8 + 4.75 * h + k

        def pe_a():
            yield 1
            pe = nc.tensor
            pe.wait_ge(A["mv"], 2)
            mm(project_bank[:, 0:2], mean_of_all[:, :], mv_a[:, :, 0], start=True, stop=True).then_inc(A["mean_ps"], 1)
            yield 3
            pe.wait_ge(A["var"], 1)
            mm(project_bank[:, 2:4], mean_of_all[:, :], small_a[:, 3, :], start=True, stop=True).then_inc(A["var_ps"], 1)
            yield 6
            pe.wait_ge(A["csplit"], 1)
            pe.wait_ge(A["eps"], 1)
            for n in range(2):
                for kt in range(KT):
                    if n or kt:
                        yield 6
                    ps = (*scores_bank, transposed_bank, project_bank)[2 * n + kt]
                    lhs = c_split[:, n, kt * P:(kt + 1) * P]
                    mm(ps[:, :], lhs, wvo_hi[:, :], start=True, stop=False)
                    mm(ps[:, :], lhs, wvo_lo[:, :], start=False, stop=True).then_inc(A["v_ps"], 1)
            def project(h):
                if h == 0:
                    pe.wait_ge(A["v_sb"], 4)
                    pe.wait_ge(A["xlo"], 1)
                else:
                    pe.wait_ge(A["k_lo"], h)
                mm(project_bank[:, :], wq_split[:, h, :], x_hi[:, :, :], start=True, stop=False)
                mm(project_bank[:, :], wq_split[:, h, :], x_lo[:, :, :], start=False, stop=True).then_inc(A["q_ps"], 1)

            def project_keys(h):
                pe.wait_ge(A["q_lo"], h + 1)
                mm(project_bank[:, :], wk_split[:, h, :], c_hi[:, :, :], start=True, stop=False)
                mm(project_bank[:, :], wk_split[:, h, :], c_lo[:, :, :], start=False, stop=True).then_inc(A["k_ps"], 1)

            def score(h, n):
                pe.wait_ge(A["k_lo"], h + 1)
                if h:
                    pe.wait_ge(A["exp"], 2 * h - 1 + n)
                for qt in range(KT):
                    lhs = q_split[:, n, qt * P:(qt + 1) * P]
                    ps = scores_bank[n][:, qt * D:(qt + 1) * D]
                    mm(ps, lhs, k_hi[:, n, :], start=True, stop=False)
                    last = mm(ps, lhs, k_lo[:, n, :], start=False, stop=True)
                last.then_inc(A["scores"], 1)

            def transpose(h, n):
                pe.wait_ge(A["prob"], 2 * h + n + 1)
                if n:
                    pe.wait_ge(A["pt0"], h + 1)
                elif h:
                    pe.wait_ge(A["pt1"], h)
                for qt in range(KT):
                    for kt in range(KT):
                        last = nc.tensor.transpose(transposed_bank[:, kt * D + qt * P:kt * D + (qt + 1) * P],
                                                   p_a[:, n, qt, kt * P:(kt + 1) * P], ident[:, :])
                last.then_inc(A["trans"], 1)

            def attend(h):
                pe.wait_ge(A["pt0"], h + 1)
                pe.wait_ge(A["pt1"], h + 1)
                for kt in range(KT):
                    for n in range(2):
                        last = mm(attended_bank[n * S:(n + 1) * S, 0:D], v_a[:, n, kt, h * S:(h + 1) * S], pt_a[:, n, kt, :],
                                  start=h == 0 and kt == 0, stop=h == H0 - 1 and kt == KT - 1)
                last.then_inc(A["att"], 1)

            yield head_step(0)
            project(0)
            yield head_step(0, 0.5)
            project_keys(0)
            yield head_step(0, 1)
            score(0, 0)
            yield head_step(0, 1)
            score(0, 1)
            for h in range(H0):
                if h + 1 < H0:
                    yield head_step(h, 1.75)
                    project(h + 1)
                    yield head_step(h, 2.5)
                    project_keys(h + 1)
                yield head_step(h, 3.5)
                transpose(h, 0)
                yield head_step(h, 4)
                transpose(h, 1)
                if h + 1 < H0:
                    yield head_step(h, 4.75)
                    score(h + 1, 0)
                    yield head_step(h, 4.8)
                    score(h + 1, 1)
                yield head_step(h, 5.25)
                attend(h)

        def dve_a(b_runs):
            dve = nc.vector
            yield 0
            for n in range(2):
                dve.bn_stats(stats_a[:, n, :], x_dup[:, n, :]).then_inc(A["stats"], 1)
            dve.wait_ge(A["stats"], 2)
            for n in range(2):
                dve.bn_aggr(mv_a[:, n, :], stats_a[:, n, :]).then_inc(A["mv"], 1)
            yield 2
            mean, dev, sq, var, eps, scale, shift, bias = (small_a[:, j, :] for j in range(8))
            dve.wait_ge(A["mean_ps"], 1)
            dve.tensor_copy(mean, project_bank[:, 0:2]).then_inc(A["mean"], 1)
            dve.wait_ge(A["mean"], 1)
            dve.tensor_tensor(dev, mv_a[:, :, 0], mean, ALU.subtract).then_inc(A["dev"], 1)
            dve.wait_ge(A["dev"], 1)
            dve.tensor_tensor(sq, dev, dev, ALU.mult).then_inc(A["sq"], 1)
            dve.wait_ge(A["sq"], 1)
            dve.tensor_tensor(var, sq, mv_a[:, :, 1], ALU.add).then_inc(A["var"], 1)
            yield 4
            dve.wait_ge(A["chi"], 1)
            dve.tensor_tensor(c_lo[:, :, :], c_dup[:, :, :], c_hi[:, :, :].bitcast(F32), ALU.subtract).then_inc(A["clo"], 1)
            dve.tensor_copy(c_split[0:S, :, :], c_dup[0:S, :, :])
            dve.tensor_tensor(c_split[S:P, :, :], c_dup[S:P, :, :], c_hi[S:P, :, :].bitcast(F32), ALU.subtract).then_inc(A["csplit"], 1)
            yield 4.2
            dve.wait_ge(A["var_ps"], 1)
            dve.tensor_scalar(eps, project_bank[:, 2:4], 1e-5, None, ALU.add).then_inc(A["eps"], 1)
            yield 5
            dve.wait_ge(A["rstd"], 1)
            dve.tensor_scalar(scale, bias, col("l0_gamma"), None, ALU.mult).then_inc(A["scale"], 1)
            dve.wait_ge(A["scale"], 1)
            dve.tensor_tensor(shift, mean, scale, ALU.mult).then_inc(A["shift"], 1)
            dve.wait_ge(A["shift"], 1)
            dve.tensor_scalar(bias, shift, -1.0, col("l0_beta"), ALU.mult, ALU.add).then_inc(A["bias"], 1)
            dve.wait_ge(A["bias"], 1)
            for n in range(2):
                dve.tensor_scalar(xn_a[:, n, :], x_dup[:, n, :], scale[:, n:n + 1], bias[:, n:n + 1], ALU.mult, ALU.add).then_inc(A["norm"], 1)
            yield 7
            dve.wait_ge(A["xhi"], 1)
            dve.tensor_tensor(x_lo[:, :, :], xn_a[:, :, :], x_hi[:, :, :].bitcast(F32), ALU.subtract).then_inc(A["xlo"], 1)

            def low_queries(h):
                dve.wait_ge(A["q_hi"], h + 1)
                dve.scalar_tensor_tensor(q_split[S:P, :, :], project_bank[S:P, :], col("l0_bq")[S:P, h:h + 1],
                                         q_split[S:P, :, :].bitcast(F32), ALU.add, ALU.subtract).then_inc(A["q_lo"], 1)

            def low_keys(h):
                dve.wait_ge(A["k_hi"], h + 1)
                if h:
                    dve.wait_ge(A["scores"], 2 * h)
                dve.scalar_tensor_tensor(k_lo[:, :, :], project_bank[:, :], col("l0_bk")[:, h:h + 1],
                                         k_hi[:, :, :].bitcast(F32), ALU.add, ALU.subtract).then_inc(A["k_lo"], 1)

            def maxima(h, n):
                dve.wait_ge(A["scores"], 2 * h + n + 1)
                dve.tensor_reduce(max_a[:, n, :], scores_bank[n][:, :].rearrange("p (q k) -> p q k", q=KT), AX.X, ALU.max).then_inc(A["max"], 1)
                dve.wait_ge(A["max"], 2 * h + n + 1)
                if h:
                    dve.wait_ge(A["exp"], 2 * h - 1 + n)
                dve.tensor_scalar(nmax_a[:, n, :], max_a[:, n, :], -(S ** -0.5), None, ALU.mult).then_inc(A["nmax"], 1)

            yield head_step(0, 0.25)
            low_queries(0)
            yield head_step(0, 0.75)
            low_keys(0)
            yield head_step(0, 1.25)
            maxima(0, 0)
            yield head_step(0, 1.25)
            maxima(0, 1)
            for h in range(H0):
                for n in range(2):
                    yield head_step(h, 2)
                    dve.wait_ge(A["exp"], 2 * h + n + 1)
                    dve.reciprocal(rec_a[:, n, :], sum_a[:, n, :]).then_inc(A["rec"], 1)
                if h + 1 < H0:
                    yield head_step(h, 2.25)
                    low_queries(h + 1)
                    yield head_step(h, 3)
                    low_keys(h + 1)
                yield head_step(h, 4.5)
                dve.wait_ge(A["trans"], 2 * h + 2)
                if h:
                    dve.wait_ge(A["att"], h)
                dve.tensor_copy(pt_a[:, 1, :, :], transposed_bank[:, :].rearrange("p (k q) -> p k q", k=KT)).then_inc(A["pt1"], 1)
                if h + 1 < H0:
                    yield head_step(h, 5)
                    maxima(h + 1, 0)
                    yield head_step(h, 5.3)
                    maxima(h + 1, 1)
            yield head_step(H0, 2)
            dve.wait_ge(A["att"], H0)
            dve.wait_ge(A["res"], 1)
            if b_runs:
                dve.wait_ge(B.full[0], 1)
                dve.wait_ge(B.s["res"], 1)
            dve.tensor_tensor(x1[:, :], attended_bank[:, 0:D], res_a[:, :], ALU.add).then_inc(A["x1"], 1)

        def act_a():
            act = nc.scalar
            yield 0
            act.activation(c_hi[:, :, :], c_dup[:, :, :], ACT.Copy).then_inc(A["chi"], 1)
            yield 6
            act.wait_ge(A["norm"], 2)
            act.activation(x_hi[:, :, :], xn_a[:, :, :], ACT.Copy).then_inc(A["xhi"], 1)
            for n in range(2):
                for kt in range(KT):
                    yield 6.2
                    act.wait_ge(A["v_ps"], 2 * n + kt + 1)
                    act.activation(v_a[:, n, kt, :], (*scores_bank, transposed_bank, project_bank)[2 * n + kt][:, :], ACT.Copy).then_inc(A["v_sb"], 1)

            def high_queries(h):
                act.wait_ge(A["q_ps"], h + 1)
                if h:
                    act.wait_ge(A["scores"], 2 * h)
                act.activation(q_split[:, :, :], project_bank[:, :].rearrange("p (n s) -> p n s", n=2), ACT.Identity,
                               bias=col("l0_bq")[:, h:h + 1]).then_inc(A["q_hi"], 1)

            def high_keys(h):
                act.wait_ge(A["k_ps"], h + 1)
                if h:
                    act.wait_ge(A["scores"], 2 * h)
                act.activation(k_hi[:, :, :], project_bank[:, :].rearrange("p (n s) -> p n s", n=2), ACT.Identity,
                               bias=col("l0_bk")[:, h:h + 1]).then_inc(A["k_hi"], 1)

            def exponentials(h, n):
                act.wait_ge(A["nmax"], 2 * h + n + 1)
                if h:
                    act.wait_ge(A["trans"], 2 * h - 1 + n)
                    act.wait_ge(A["rec"], 2 * h - 1 + n)
                for qt in range(KT):
                    last = act.activation(p_a[:, n, qt, :], scores_bank[n][:, qt * D:(qt + 1) * D], ACT.Exp, scale=S ** -0.5,
                                          bias=nmax_a[:, n, qt:qt + 1], accum_out=sum_a[:, n, qt:qt + 1])
                last.then_inc(A["exp"], 1)

            yield head_step(0, 0.25)
            high_queries(0)
            yield head_step(0, 0.75)
            high_keys(0)
            yield head_step(0, 1.5)
            exponentials(0, 0)
            yield head_step(0, 1.5)
            exponentials(0, 1)
            for h in range(H0):
                if h + 1 < H0:
                    yield head_step(h, 2)
                    high_queries(h + 1)
                    yield head_step(h, 2.75)
                    high_keys(h + 1)
                yield head_step(h, 3.75)
                act.wait_ge(A["trans"], 2 * h + 1)
                if h:
                    act.wait_ge(A["att"], h)
                act.activation(pt_a[:, 0, :, :], transposed_bank[:, :].rearrange("p (k q) -> p k q", k=KT), ACT.Copy).then_inc(A["pt0"], 1)
                if h + 1 < H0:
                    yield head_step(h, 5.5)
                    exponentials(h + 1, 0)
                    yield head_step(h, 5.8)
                    exponentials(h + 1, 1)

        def pool_a():
            pool = nc.gpsimd
            yield 0
            pool.tensor_scalar(res_a[:, :], x_nat[:, :], out_bias0[:, :], 1.0, ALU.add, ALU.mult).then_inc(A["res"], 1)
            yield 4.5
            pool.wait_ge(A["eps"], 1)
            pool.tensor_tensor(small_a[:, 7, :], small_a[:, 4, :], minus_half[:, :], ALU.pow).then_inc(A["rstd"], 1)
            for h in range(H0):
                for n in range(2):
                    yield head_step(h, 2.25)
                    pool.wait_ge(A["rec"], 2 * h + n + 1)
                    for qt in range(KT):
                        last = pool.tensor_scalar(p_a[:, n, qt, :], p_a[:, n, qt, :], rec_a[:, n, qt:qt + 1], 1.0, ALU.mult, ALU.mult)
                    last.then_inc(A["prob"], 1)

        ATT = 11

        def unit(T, a, f, c, blocks):
            before = (T.blocks[0] * KT) if a else 0
            return before + f * blocks + c + 1

        B.blocks, C.blocks = (1, 2), (1, 1)

        def pe_transposes(T, name, srcs):
            ps = fill_bank(T, nc.tensor, name)
            n = 0
            for src in srcs:
                for k in range(KT):
                    last = nc.tensor.transpose(ps[:, n * P:(n + 1) * P], src[:, k * P:(k + 1) * P], ident[:, :])
                    n += 1
            filled(T, last, name)

        def pe_project_T(T, name, w, srcT):
            ps = fill_bank(T, nc.tensor, name)
            for m in range(KT):
                for k in range(KT):
                    last = mm(ps[:, m * P:(m + 1) * P], w[:, k, m * P:(m + 1) * P], srcT[:, k, :], start=k == 0, stop=k == KT - 1)
            filled(T, last, name)

        def pe_values(T, name, w, srcT):
            ps = fill_bank(T, nc.tensor, name)
            wv = w.rearrange("p k (g e d) -> p k g e d", e=2, d=HD)
            for b in range(2):
                for k in range(KT):
                    for e in range(2):
                        last = mm(ps[e * S:(e + 1) * S, b * P:(b + 1) * P], srcT[:, k, b * S:(b + 1) * S], wv[:, k, :, e, :],
                                  start=k == 0, stop=k == KT - 1)
            filled(T, last, name)

        def written(T, eng, name):
            n = T.fills[name]
            eng.wait_ge(T.free[n % len(T.banks)], n // len(T.banks) + 1)

        def pe_attention(T, a, base):
            pe, blocks = nc.tensor, T.blocks[a]
            for f in range(KT):
                for c in range(blocks):
                    yield base + 1 + f + 0.5 * c
                    written(T, pe, (a, "q"))
                    pe.wait_ge(T.s["kblk"], unit(T, a, f, c, blocks))
                    ps = fill_bank(T, pe, (a, "s", f, c))
                    for b in range(2):
                        last = mm(ps[b * S:(b + 1) * S, :], T.qT[:, f, b * S:(b + 1) * S], T.kblk[:, f, c, b, :, :], start=True, stop=True)
                    filled(T, last, (a, "s", f, c))
            for f in range(KT):
                p = T.p[:, f, 0:HB * blocks * S].rearrange("p (c m) -> p c m", c=blocks)
                for c in range(blocks):
                    yield base + 6 + 1.5 * f + 0.5 * c
                    pe.wait_ge(T.s["prob"], 2 * a + f + 1)
                    ps = fill_bank(T, pe, (a, "t", f, c))
                    for g in range(HB // 2):
                        last = nc.tensor.transpose(ps[:, g * P:(g + 1) * P], p[:, c, g * P:(g + 1) * P], ident[:, :])
                    filled(T, last, (a, "t", f, c))
                yield base + 7.4 + 1.5 * f
                for c in range(blocks):
                    written(T, pe, (a, "v", c))
                    written(T, pe, (a, "t", f, c))
                ps = fill_bank(T, pe, (a, "o", f))
                for b in range(2):
                    for c in range(blocks):
                        for g in range(HB // 2):
                            last = mm(ps[32 * g:32 * (g + 1), b * S:(b + 1) * S], T.v[:, c, b, f * (HB // 2) + g, :, :],
                                      T.pt[:, f, c, g, b * S:(b + 1) * S], start=c == 0, stop=c == blocks - 1)
                filled(T, last, (a, "o", f))
            yield base + 10
            for f in range(KT):
                written(T, pe, (a, "o", f))
            ps = fill_bank(T, pe, (a, "p"))
            for f in range(KT):
                last = mm(ps[:, 0:D], T.yT[:, f, :], T.W[f"o{a}"][:, f, :], start=f == 0, stop=f == KT - 1)
            filled(T, last, (a, "p"))

        def dve_attention(T, a, base, masked):
            dve, blocks = nc.vector, T.blocks[a]

            def view(f):
                return T.p[:, f, 0:HB * blocks * S].rearrange("p (c h k) -> p c h k", c=blocks, h=HB)

            def per_head(ap):
                return bc(bc(ap, 2, S), 1, blocks)

            def whole_rows(f):
                return view(f).rearrange("p c h k -> p h c k")

            for f in range(KT):
                i = 2 * a + f + 1
                for c in range(blocks):
                    yield base + 1.5 + f + 0.5 * c
                    ps = wait_fill(T, dve, (a, "s", f, c))
                    ins = masked(c, ps[:, :].rearrange("p (h k) -> p h k", h=HB), view(f)[:, c, :, :])
                    release(T, ins, (a, "s", f, c))
                yield base + 2.4 + f
                if T is C:
                    dve.wait_ge(T.s["madd"], i)
                else:
                    for c in range(blocks):
                        written(T, dve, (a, "s", f, c))
                dve.tensor_reduce(T.max[:, f, :], whole_rows(f), AX.XY, ALU.max).then_inc(T.s["max"], 1)
                dve.wait_ge(T.s["max"], i)
                dve.tensor_tensor(view(f), view(f), per_head(T.max[:, f, :]), ALU.subtract).then_inc(T.s["sub"], 1)
            for f in range(KT):
                i = 2 * a + f + 1
                yield base + 4.5 + f
                dve.wait_ge(T.s["exp"], i)
                dve.tensor_reduce(T.sum[:, f, :], whole_rows(f), AX.XY, ALU.add).then_inc(T.s["sum"], 1)
                dve.wait_ge(T.s["sum"], i)
                dve.reciprocal(T.rec[:, f, :], T.sum[:, f, :]).then_inc(T.s["rec"], 1)
            yield base + 10.5
            ps = wait_fill(T, dve, (a, "p"))
            dve.wait_ge(T.s["res"], a + 1)
            ins = dve.tensor_tensor(T.mid[:, a, :], ps[:, 0:D], T.res[:, :], ALU.add)
            release(T, ins, (a, "p"))

        def act_attention(T, a, base):
            act, blocks = nc.scalar, T.blocks[a]
            for f in range(KT):
                yield base + 3.5 + f
                p = T.p[:, f, 0:HB * blocks * S]
                act.wait_ge(T.s["sub"], 2 * a + f + 1)
                act.activation(p, p, ACT.Exp).then_inc(T.s["exp"], 1)
            for f in range(KT):
                for c in range(blocks):
                    yield base + 6.4 + 1.5 * f + 0.5 * c
                    ps = wait_fill(T, act, (a, "t", f, c))
                    ins = act.activation(T.pt[:, f, c, :, :], ps[:, :].rearrange("p (g q) -> p g q", q=P), ACT.Copy)
                    release(T, ins, (a, "t", f, c))
                yield base + 7.8 + 1.5 * f
                ps = wait_fill(T, act, (a, "o", f))
                release(T, act.activation(T.yT[:, f, :], ps[:, 0:P], ACT.Copy), (a, "o", f))

        def pool_keys(T, a, c, base, f):
            pool, blocks = nc.gpsimd, T.blocks[a]
            yield base
            written(T, pool, (a, "k", c))
            if a:
                written(T, pool, (0, "p"))
            for b in range(2):
                last = pool.tensor_tensor(T.kblk[:, f, c, b, :, :], bc(T.kT[:, c, f, b * S:(b + 1) * S], 1, HB), bc(head_mask[:, :], 2, S), ALU.mult)
            last.then_inc(T.s["kblk"], 1)

        def pool_attention(T, a, base, mask_add):
            pool, blocks = nc.gpsimd, T.blocks[a]
            for f in range(KT):
                for c in range(blocks):
                    yield from pool_keys(T, a, c, base + 0.3 * f, f)
            for f in range(KT):
                if mask_add is not None:
                    yield base + 2 + f
                    written(T, pool, (a, "s", f, 0))
                    v = T.p[:, f, 0:HB * S].rearrange("p (h k) -> p h k", h=HB)
                    pool.tensor_tensor(v, v, bc(mask_add[:, :], 1, HB), ALU.add).then_inc(T.s["madd"], 1)
            for f in range(KT):
                yield base + 5 + f
                pool.wait_ge(T.s["rec"], 2 * a + f + 1)
                v = T.p[:, f, 0:HB * blocks * S].rearrange("p (c h k) -> p c h k", c=blocks, h=HB)
                pool.tensor_tensor(v, v, bc(bc(T.rec[:, f, :], 2, S), 1, blocks), ALU.mult).then_inc(T.s["prob"], 1)

        def pool_residual(T, n, step, src, row, ready):
            yield step
            ready(nc.gpsimd)
            nc.gpsimd.tensor_tensor(T.res[:, :], src, row_bias[:, row, :], ALU.add).then_inc(T.s["res"], 1)

        def dve_norm(T, n, step, src, eps, rms=False):
            dve = nc.vector
            yield step
            dve.bn_stats(T.stats[:, :], src).then_inc(T.s["stats"], 1)
            dve.wait_ge(T.s["stats"], n + 1)
            dve.bn_aggr(T.mv[:, :], T.stats[:, :]).then_inc(T.s["mv"], 1)
            dve.wait_ge(T.s["mv"], n + 1)
            mean, var = T.mv[:, 0:1], T.mv[:, 1:2]
            if rms:
                dve.scalar_tensor_tensor(T.msq[:, :], mean, mean, var, ALU.mult, ALU.add).then_inc(T.s["msq"], 1)
                dve.wait_ge(T.s["msq"], 1)
                var = T.msq[:, :]
            dve.tensor_scalar(T.eps[:, :], var, eps, None, ALU.add).then_inc(T.s["eps"], 1)
            yield step + 2
            dve.wait_ge(T.s["rstd"], n + 1)
            if n:
                written(T, dve, f"nT{n - 1}")
            if rms:
                dve.tensor_scalar(T.xn[:, :], src, T.rstd[:, :], 1.0, ALU.mult, ALU.mult).then_inc(T.s["xn"], 1)
            else:
                dve.tensor_scalar(T.xn[:, :], src, mean, T.rstd[:, :], ALU.subtract, ALU.mult).then_inc(T.s["xn"], 1)

        def pool_norm(T, n, step):
            yield step + 1
            nc.gpsimd.wait_ge(T.s["eps"], n + 1)
            nc.gpsimd.tensor_tensor(T.rstd[:, :], T.eps[:, :], minus_half[:, 0:1], ALU.pow).then_inc(T.s["rstd"], 1)

        def pe_norm(T, n, step):
            yield step + 2.5
            nc.tensor.wait_ge(T.s["xn"], n + 1)
            pe_transposes(T, f"nT{n}", [T.xn])

        def act_copy(T, step, name, dst, width):
            yield step
            ps = wait_fill(T, nc.scalar, name)
            release(T, nc.scalar.activation(dst, ps[:, 0:width], ACT.Copy), name)

        def act_norm(T, n, step):
            yield from act_copy(T, step + 3, f"nT{n}", T.xnT[:, :, :], D)

        def act_values(T, a, c, step):
            yield step
            ps = wait_fill(T, nc.scalar, (a, "v", c))
            for e in range(2):
                last = nc.scalar.activation(T.v[e * S:(e + 1) * S, c, :, :, e, :],
                                            ps[e * S:(e + 1) * S, 0:D].rearrange("p (b g d) -> p b g d", b=2, d=HD), ACT.Copy)
            release(T, last, (a, "v", c))

        def dve_bias(T, step, name, dst, bias):
            yield step
            ps = wait_fill(T, nc.vector, name)
            n = bias.shape[1]
            ins = nc.vector.tensor_tensor(dst, ps[:, 0:n * P].rearrange("p (m t) -> p m t", t=P), bc(bias, 2, P), ALU.add)
            release(T, ins, name)

        def pe_mlp(T, n, step):
            pe = nc.tensor
            for half in range(2):
                yield step + 1.5 * half
                written(T, pe, f"nT{n}")
                ps = fill_bank(T, pe, f"h{half}")
                for m in range(MT // 2):
                    cols_ = slice((half * MT // 2 + m) * P, (half * MT // 2 + m + 1) * P)
                    for k in range(KT):
                        last = mm(ps[:, m * P:(m + 1) * P], T.W["w1"][:, k, cols_], T.xnT[:, k, :], start=k == 0, stop=k == KT - 1)
                filled(T, last, f"h{half}")
            for m in range(MT):
                if m % (MT // 2) == 0:
                    yield step + 4 + 1.5 * (m > 0)
                    pe.wait_ge(T.s["hid"], 2 * m // MT + 1)
                    if m == 0:
                        ps = fill_bank(T, pe, "y")
                last = mm(ps[:, 0:D], T.hid[:, m, :], T.W["w2"][:, m, :], start=m == 0, stop=m == MT - 1)
            filled(T, last, "y")

        def dve_mlp(T, step, bias, dst, ready):
            for half in range(2):
                m = half * MT // 2
                yield from dve_bias(T, step + 0.7 + 1.5 * half, f"h{half}", T.hid[:, m:m + MT // 2, :], bias[:, m:m + MT // 2])
            yield step + 6
            ps = wait_fill(T, nc.vector, "y")
            nc.vector.wait_ge(T.s["res"], 3)
            ready(nc.vector)
            release(T, nc.vector.tensor_tensor(dst, ps[:, 0:D], T.res[:, :], ALU.add), "y")

        def act_mlp(T, step):
            for half in range(2):
                yield step + 1 + 1.5 * half
                written(T, nc.scalar, f"h{half}")
                h = T.hid[:, half * MT // 2:(half + 1) * MT // 2, :]
                nc.scalar.activation(h, h, ACT.Gelu_apprx_tanh).then_inc(T.s["hid"], 1)

        def pe_b():
            pe = nc.tensor
            yield 0
            pe_transposes(B, "xT", [B.c, x1])
            yield from pe_norm(B, 0, 0)
            yield 3.5
            written(B, pe, "xT")
            pe_project_T(B, (0, "q"), B.W["q0"], B.xT[:, KT:2 * KT, :])
            yield 4
            written(B, pe, "nT0")
            pe_project_T(B, (0, "k", 0), B.W["k0"], B.xnT)
            yield 4.5
            pe_values(B, (0, "v", 0), B.W["v0"], B.xnT)
            yield from pe_attention(B, 0, 5)
            yield 16
            written(B, pe, (0, "p"))
            pe_transposes(B, "x2T", [B.mid[:, 0, :]])
            yield 17
            written(B, pe, "x2T")
            srcs = (B.xT[:, 0:KT, :], B.x2T)
            pe_project_T(B, (1, "q"), B.W["q1"], B.x2T)
            for c in range(2):
                yield 17.5 + 0.5 * c
                pe_project_T(B, (1, "k", c), B.W["k1"], srcs[c])
            for c in range(2):
                yield 18.5 + 0.5 * c
                pe_values(B, (1, "v", c), B.W["v1"], srcs[c])
            yield from pe_attention(B, 1, 19)
            yield from pe_norm(B, 1, 30)
            yield from pe_mlp(B, 1, 34)

        def dve_b(c_runs):
            dve = nc.vector
            yield from dve_norm(B, 0, 0, B.c[:, :], 1e-5)
            yield 3
            dve.tensor_scalar(m1[:, :], m1_raw[:, :], 0.0, NEG, ALU.is_equal, ALU.mult).then_inc(B.s["mask"], 1)
            dve.tensor_scalar(m2[:, :], m2_raw[:, :], 0.0, NEG, ALU.is_equal, ALU.mult).then_inc(B.s["mask"], 1)
            yield from dve_bias(B, 4.3, (0, "k", 0), B.kT[:, 0, :, :], fcol("bk1"))
            dve.wait_ge(B.s["mask"], 2)

            def masked(scale, mask):
                def run(c, ps, dst):
                    if mask is not None and c == 0:
                        return dve.scalar_tensor_tensor(dst, ps, scale, bc(mask[:, :], 1, HB), ALU.mult, ALU.add)
                    return dve.tensor_scalar(dst, ps, scale, None, ALU.mult)
                return run

            yield from dve_attention(B, 0, 5, masked(HD ** -0.5, m1))
            yield from dve_bias(B, 17.3, (1, "q"), B.qT[:, :, :], col("l2_bq"))
            for c in range(2):
                yield from dve_bias(B, 17.8 + 0.5 * c, (1, "k", c), B.kT[:, c, :, :], col("l2_bk"))
            yield from dve_attention(B, 1, 19, masked(1.0 / HD, m2))
            written(B, dve, (1, "p"))
            yield from dve_norm(B, 1, 30, B.mid[:, 1, :], 1e-6, rms=True)

            def x3_free(eng):
                if c_runs:
                    eng.wait_ge(C.s["xn"], 1)
                    eng.wait_ge(C.s["res"], 1)
            yield from dve_mlp(B, 34, col("l2_b1"), x3[:, :], x3_free)

        def act_b():
            yield from act_copy(B, 1, "xT", B.xT[:, :, :], 2 * D)
            yield from act_norm(B, 0, 0)
            yield from act_copy(B, 3.8, (0, "q"), B.qT[:, :, :], D)
            yield from act_values(B, 0, 0, 4.8)
            yield from act_attention(B, 0, 5)
            yield from act_copy(B, 16.5, "x2T", B.x2T[:, :, :], D)
            for c in range(2):
                yield from act_values(B, 1, c, 18.8 + 0.5 * c)
            yield from act_attention(B, 1, 19)
            yield from act_norm(B, 1, 30)
            yield from act_mlp(B, 34)

        def pool_b():
            yield from pool_residual(B, 0, 0, x1[:, :], 0, lambda pool: None)
            yield from pool_norm(B, 0, 0)
            yield from pool_attention(B, 0, 5, None)
            yield from pool_residual(B, 1, 16.5, B.mid[:, 0, :], 1, lambda pool: written(B, pool, (0, "p")))
            yield from pool_attention(B, 1, 19, None)
            yield from pool_norm(B, 1, 30)
            yield from pool_residual(B, 2, 31.5, B.mid[:, 0, :], 2, lambda pool: written(B, pool, (1, "p")))

        def pe_c():
            pe = nc.tensor
            yield 0
            pe_transposes(C, "xT", [C.c])
            yield from pe_norm(C, 0, 0)
            yield 3.5
            written(C, pe, "nT0")
            pe_project_T(C, (0, "q"), C.W["q0"], C.xnT)
            yield 4
            pe_project_T(C, (0, "k", 0), C.W["k0"], C.xnT)
            yield 4.5
            pe_values(C, (0, "v", 0), C.W["v0"], C.xnT)
            yield from pe_attention(C, 0, 5)
            yield from pe_norm(C, 1, 16)
            yield 19.5
            written(C, pe, "nT1")
            pe_project_T(C, (1, "q"), C.W["q1"], C.xnT)
            yield 20
            written(C, pe, "xT")
            pe_project_T(C, (1, "k", 0), C.W["k1"], C.xT)
            yield 20.5
            pe_values(C, (1, "v", 0), C.W["v1"], C.xT)
            yield from pe_attention(C, 1, 21)
            yield from pe_norm(C, 2, 32)
            yield from pe_mlp(C, 2, 36)

        def dve_c():
            dve = nc.vector
            yield from dve_norm(C, 0, 0, x3[:, :], 1e-5)
            yield 3
            dve.tensor_scalar(m4_mul[:, :], m4_raw[:, :], HD ** -0.5, None, ALU.mult).then_inc(C.s["mask"], 1)
            dve.tensor_scalar(m4_add[:, :], m4_raw[:, :], 10000.0, -10000.0, ALU.mult, ALU.add).then_inc(C.s["mask"], 1)
            yield from dve_bias(C, 3.8, (0, "q"), C.qT[:, :, :], fcol("q3"))
            yield from dve_bias(C, 4.3, (0, "k", 0), C.kT[:, 0, :, :], fcol("k3"))
            dve.wait_ge(C.s["mask"], 2)

            def masked(mask):
                return lambda c, ps, dst: dve.tensor_tensor(dst, ps, bc(mask[:, :], 1, HB), ALU.mult)

            yield from dve_attention(C, 0, 5, masked(self_mul))
            written(C, dve, (0, "p"))
            yield from dve_norm(C, 1, 16, C.mid[:, 0, :], 1e-5)
            yield from dve_bias(C, 19.8, (1, "q"), C.qT[:, :, :], fcol("q4"))
            yield from dve_bias(C, 20.3, (1, "k", 0), C.kT[:, 0, :, :], col("l3_bk"))
            yield from dve_attention(C, 1, 21, masked(m4_mul))
            written(C, dve, (1, "p"))
            yield from dve_norm(C, 2, 32, C.mid[:, 1, :], 1e-5)
            yield from dve_mlp(C, 36, fcol("b1"), y_out[:, :], lambda eng: eng.wait_ge(stored, 16))

        def act_c():
            yield from act_copy(C, 1, "xT", C.xT[:, 0:KT, :], D)
            yield from act_norm(C, 0, 0)
            yield from act_values(C, 0, 0, 4.8)
            yield from act_attention(C, 0, 5)
            yield from act_norm(C, 1, 16)
            yield from act_values(C, 1, 0, 20.8)
            yield from act_attention(C, 1, 21)
            yield from act_norm(C, 2, 32)
            yield from act_mlp(C, 36)

        def pool_c():
            yield from pool_residual(C, 0, 0, x3[:, :], 3, lambda pool: None)
            yield from pool_norm(C, 0, 0)
            yield from pool_attention(C, 0, 5, self_add)
            yield from pool_residual(C, 1, 16.5, C.mid[:, 0, :], 4, lambda pool: written(C, pool, (0, "p")))
            yield from pool_norm(C, 1, 16)
            yield 20
            nc.gpsimd.wait_ge(C.s["mask"], 2)
            yield from pool_attention(C, 1, 21, m4_add)
            yield from pool_residual(C, 2, 32.5, C.mid[:, 1, :], 5, lambda pool: written(C, pool, (1, "p")))
            yield from pool_norm(C, 2, 32)

        def running(a, b, c, program_a, program_b, program_c):
            return {name: program() for name, runs, program in (("a", a, program_a), ("b", b, program_b), ("c", c, program_c)) if runs}

        def body(i, a, b, c, load_next=True, store=True):
            with nc.Block() as block:

                @block.sync
                def _(sp):
                    n = 0
                    if c and store:
                        sp.dma_start(out[pair(i - 3)].rearrange("n c s -> (n c) s"), y_out[:, :]).then_inc(stored, 16)
                    elif c:
                        sp.sem_inc(stored, 16)
                    if b and a:
                        sp.wait_ge(B.full[0], 1)
                        sp.wait_ge(B.s["xn"], 1)
                        sp.wait_ge(B.s["mask"], 2)
                    if a:
                        n += load_b(sp, i)
                    if c and b:
                        sp.wait_ge(C.full[0], 1)
                        sp.wait_ge(C.s["mask"], 2)
                    if b:
                        n += load_c(sp, i - 1)
                    if a and load_next:
                        sp.wait_ge(A["csplit"], 1)
                        sp.wait_ge(A["norm"], 2)
                        sp.wait_ge(A["res"], 1)
                        n += load_a(sp, i + 1)
                    if n:
                        sp.wait_ge(loaded, n)
                    if c:
                        sp.wait_ge(stored, 16)

                @block.gpsimd
                def _(pool):
                    weave("pool", running(a, b, c, pool_a, pool_b, pool_c))

                @block.tensor
                def _(pe):
                    weave("pe", running(a, b, c, pe_a, pe_b, pe_c))

                @block.scalar
                def _(act):
                    weave("act", running(a, b, c, act_a, act_b, act_c))

                @block.vector
                def _(dve):
                    weave("dve", running(a, b, c, lambda: dve_a(b), lambda: dve_b(c), dve_c))

            nc.all_engine_barrier(sems_to_clear=clear)

        body(0, True, False, False)
        body(1, True, True, False)
        body(2, True, True, True, store=False)
        with nc.Fori(3, PAIRS - 1) as i:
            body(i, True, True, True)
        body(PAIRS - 1, True, True, True, load_next=False)
        body(PAIRS, False, True, True)
        body(PAIRS + 1, False, False, True)
        with nc.Block() as block:

            @block.sync
            def _(sp):
                sp.dma_start(out[pair(PAIRS - 1)].rearrange("n c s -> (n c) s"), y_out[:, :]).then_inc(stored, 16)
                sp.wait_ge(stored, 16)


def _dup(a):
    return np.concatenate([a, a], 0)


def _blocks(a):
    r, n = a.shape
    return np.ascontiguousarray(a.reshape(r // P, P, n).transpose(1, 0, 2).reshape(P, -1))


def kernel(**inputs):
    import concourse.bacc as bacc
    from concourse.bass_utils import run_bass_kernel_spmd

    g = {k: np.asarray(v) for k, v in inputs.items()}
    L0, L1, L2, L3 = ({k.split("_xattn_")[1]: v for k, v in g.items() if k.startswith(f"L{n}_xattn_")} for n in range(4))
    col = lambda v: np.ascontiguousarray(v.reshape(-1, P).T)
    parts = {
        "l0_gamma": _dup(L0["gamma"])[:, None], "l0_beta": _dup(L0["beta"])[:, None], "l0_bo": _dup(L0["bo"])[:, None],
        "l0_bq": _dup(L0["bq"].reshape(H0, S).T), "l0_bk": _dup(L0["bkv"][:H0 * S].reshape(H0, S).T),
        "l1_g": col(L1["ln_gamma"]), "l1_b": col(L1["ln_beta"]),
        "l2_bq": col(L2["q_b"]), "l2_bk": col(L2["kv_b"][0::2]), "l2_bv": col(L2["kv_b"][1::2]),
        "l2_post": col(L2["postnorm_w"]), "l2_b1": col(L2["mlp_b1"]),
        "l3_g1": col(L3["ln1_s"]), "l3_b1n": col(L3["ln1_b"]), "l3_bqkv": col(L3["b_qkv"]),
        "l3_g2": col(L3["ln2_s"]), "l3_b2n": col(L3["ln2_b"]), "l3_bq": col(L3["b_q"]),
        "l3_bk": col(L3["b_kv"][:D]), "l3_bv": col(L3["b_kv"][D:]),
        "l3_g3": col(L3["ln3_s"]), "l3_b3n": col(L3["ln3_b"]), "l3_b1": col(L3["b1"]),
    }
    wide = lambda w: np.stack([w, w], 2).reshape(w.shape[0], H0 * P)
    heads_T = lambda w: w.T.reshape(S, H0, S)
    wqkv, wkv3 = L3["w_qkv"], L3["w_kv"]
    arrays = {
        "x": g["x"], "ctx": g["ctx_2048"],
        "mask1": g["mask_BxS2_bf1"].view(np.uint8), "mask2": g["mask_BxS2_ik0"],
        "self_mask": g["mask_1x1xSxS2_fc1"].reshape(S, S), "mask4": g["mask_Bx1xSxS2_ff1"].reshape(NSEQ, S, S),
        "cols": np.concatenate([parts[n] for n in COLS], 1),
        "rows": np.stack([L2["out_b"], L2["mlp_b2"], L3["b_ao"], L3["b_co"], L3["b2"]]),
        "gate": L1["gate"],
        "wq0": _dup(wide(heads_T(L0["Wq"]))), "wk0": _dup(wide(heads_T(L0["Wkv"][:H0 * S]))),
        "wv0": wide(L0["Wkv"][H0 * S:].reshape(H0, S, S).transpose(1, 0, 2)),
        "wo0": np.ascontiguousarray(L0["Wo"].reshape(S, H0, S).transpose(2, 1, 0)).reshape(S, H0 * S),
        "bv0": np.ascontiguousarray(L0["bkv"][H0 * S:].reshape(H0, S).T),
        "wb": np.concatenate([_blocks(w) for w in (L1["Wq"].T, L1["Wk"].T, L1["Wv"].T, L1["Wo"].T, L2["q_w"], L2["kv_w"][:, 0::2],
                                                   L2["kv_w"][:, 1::2], L2["out_w"], L2["mlp_w1"], L2["mlp_w2"])], 1),
        "wc": np.concatenate([_blocks(w) for w in (wqkv[:, :D], wqkv[:, D:2 * D], wqkv[:, 2 * D:], L3["w_ao"], L3["w_q"], wkv3[:, :D],
                                                   wkv3[:, D:], L3["w_co"], L3["w1"], L3["w2"])], 1),
    }
    arrays = {f"in_{n}": np.ascontiguousarray(a) for n, a in arrays.items()}
    nc = bacc.Bacc("TRN2", target_bir_lowering=False, num_devices=1)
    dram = {n[3:]: nc.dram_tensor(n, a.shape, mybir.dt.from_np(a.dtype), kind="ExternalInput").ap() for n, a in arrays.items()}
    out = nc.dram_tensor("out", (NSEQ, S, D), F32, kind="ExternalOutput").ap()
    build(nc, dram, out)
    got = run_bass_kernel_spmd(nc, [arrays], core_ids=[0])
    return got.results[0]["out"]
```

```python
from contextlib import ExitStack

import numpy as np
import concourse.bass as bass
from concourse import mybir

F32 = mybir.dt.float32
F32R = mybir.dt.float32r
U8 = mybir.dt.uint8
I32 = mybir.dt.int32
ALU = mybir.AluOpType
ACT = mybir.ActivationFunctionType
AX = mybir.AxisListType

P = 128
NSEQ, S, D = 32, 64, 256
PAIRS = NSEQ // 2
KT = D // P
H0 = 8
HEADS, HD = 16, 16
HB = HEADS // KT
HID = 4 * D
MT = HID // P
NEG = -1.0e30

COLS = {}
for _name, _n in (("l0_gamma", 1), ("l0_beta", 1), ("l0_bo", 1), ("l0_bq", H0), ("l0_bk", H0),
                  ("l1_g", KT), ("l1_b", KT),
                  ("l2_bq", KT), ("l2_bk", KT), ("l2_bv", KT), ("l2_post", KT), ("l2_b1", MT),
                  ("l3_g1", KT), ("l3_b1n", KT), ("l3_bqkv", 3 * KT), ("l3_g2", KT), ("l3_b2n", KT),
                  ("l3_bq", KT), ("l3_bk", KT), ("l3_bv", KT), ("l3_g3", KT), ("l3_b3n", KT), ("l3_b1", MT)):
    COLS[_name] = (sum(n for _, n in COLS.values()), _n)
NCOLS = sum(n for _, n in COLS.values())
ROWS = ["l2_bo", "l2_b2", "l3_bao", "l3_bco", "l3_b2"]

WB = {"q0": (KT, D), "k0": (KT, D), "v0": (KT, D), "o0": (KT, D),
      "q1": (KT, D), "k1": (KT, D), "v1": (KT, D), "o1": (KT, D), "w1": (KT, HID), "w2": (MT, D)}
WC = dict(WB)
WCOLS = sum(a * b for a, b in WB.values())

def attention_fills(a, blocks):
    return ([(a, "s", f, c) for f in range(KT) for c in range(blocks)]
            + [x for f in range(KT) for x in [(a, "t", f, c) for c in range(blocks)] + [(a, "o", f)]]
            + [(a, "p")])


FILLS_B = (["xT", "nT0"] + [(0, "q"), (0, "k", 0), (0, "v", 0)] + attention_fills(0, 1) + ["x2T"]
           + [(1, "q"), (1, "k", 0), (1, "k", 1), (1, "v", 0), (1, "v", 1)] + attention_fills(1, 2)
           + ["nT1", "h0", "h1", "y"])
FILLS_C = (["xT", "nT0"] + [(0, "q"), (0, "k", 0), (0, "v", 0)] + attention_fills(0, 1)
           + ["nT1"] + [(1, "q"), (1, "k", 0), (1, "v", 0)] + attention_fills(1, 1)
           + ["nT2", "h0", "h1", "y"])


ORDER = {
    "ab": {
        "pool": "bbaabbbbaabaabbaabbaaababaaababaa",
        "pe": "babababaaabababaaababbaabaababaabaaabaababaabaaaababaabaaabaaaaaaababaababaaabababaaaababaababab",
        "act": "abbbaaaaabaabbaabaabbbaaaabaaaaaabbaaaaabaaaaabaaabababbaabaabaabaabab",
        "dve": "babaaabaababbbabbaaabaaaaabaaaabaaababaaaaaaabaababbaaabaabaabaaabaaaaaaaaaababaabaaaabbaab",
    },
    "abc": {
        "pool": "bbacacbbccbcbacaccababbbaccabccacabcbacaccaabbccaaaa",
        "pe": "bcabababacbaabcacbaccaaababcbabaaababababcabcaaacbacabcabaabaacbaccabcaacaaacababababaaababaabcaaccaacabcabacaacabacababcaca",
        "act": "bacbbaabcaaaabacbaabaabcbbaacbaaacacacbacabaaacabaabacaaababbcbaabacbaacccaacabaacbaaccbaa",
        "dve": "babaaaccacbbabbccabbabcaaabcaacaaacbaacbcaabbaaaaaccaaabaabcbacbcaabababaacaabaaccaaacaaccabaabaabaacccabaacaaabcaaabca",
    },
    "bc": {
        "pool": "bbccbbccbcbccbcbcbcbbccccbcbccccbb",
        "pe": "cbbbcbcbcbcbccbbbbbbcbccbcbbcbbbcbccbcccbbbcbccbccbbccbcbcbcbb",
        "act": "bbcbcbbbcbbbcbcbccccbbcbbccbbcbccbcbcbcbccbb",
        "dve": "bcbbccbccbbbbbcbccccbcbbbccbcbbbccbbcbccbccccccbbbccbbcb",
    },
}
LENGTH = {"a": 47.0, "b": 41.0, "c": 43.0, "s": 47.0}


def weave(engine, programs):
    order = ORDER.get("".join(programs))
    if order:
        for program in programs.values():
            next(program)
        for stage in order[engine]:
            next(programs[stage], None)
        return
    waiting = []
    for name, program in programs.items():
        waiting.append([next(program) / LENGTH[name], name, program])
    while waiting:
        first = min(waiting, key=lambda w: (w[0], w[1]))
        step = next(first[2], None)
        if step is None:
            waiting.remove(first)
        else:
            first[0] = max(first[0], step / LENGTH[first[1]])


class Stage:
    pass


def build(nc, dram, out):
    ctx = ExitStack()
    with ctx:
        sb = lambda name, shape, dt=F32: ctx.enter_context(nc.sbuf_tensor(name, shape, dt))
        bank = lambda name: ctx.enter_context(nc.psum_tensor(name, [P, 512], F32))
        sems = []

        def sem(name):
            sems.append(ctx.enter_context(nc.semaphore(name)))
            return sems[-1]

        ident = sb("ident", [P, P])
        mean_of_all = sb("mean_of_all", [P, P])
        minus_half = sb("minus_half", [P, 2])
        head_mask = sb("head_mask", [P, HB])
        cols = sb("cols", [P, NCOLS])
        col = lambda name: cols[:, COLS[name][0]:COLS[name][0] + COLS[name][1]]
        gate = sb("gate", [P, 1])
        tanh_gate = sb("tanh_gate", [P, 1])
        bv_raw = sb("bv_raw", [S, H0])
        wq_split = sb("wq_split", [P, H0, P], F32R)
        wk_split = sb("wk_split", [P, H0, P], F32R)
        wvo_hi = sb("wvo_hi", [P, H0 * S], F32R)
        wvo_lo = sb("wvo_lo", [P, H0 * S], F32R)
        out_bias0 = sb("out_bias0", [P, 1])
        wb = sb("wb", [P, WCOLS])
        wc = sb("wc", [P, WCOLS])

        def weights(tile, table):
            got, at = {}, 0
            for name, (a, b) in table.items():
                got[name] = tile[:, at:at + a * b].rearrange("p (a b) -> p a b", a=a)
                at += a * b
            return got

        WBt, WCt = weights(wb, WB), weights(wc, WC)
        fold = sb("fold", [P, 20])
        FOLD = {"bk1": (0, KT), "bv1": (2, KT), "q3": (4, KT), "k3": (6, KT), "v3": (8, KT), "q4": (10, KT), "b1": (12, MT)}
        fcol = lambda name: fold[:, FOLD[name][0]:FOLD[name][0] + FOLD[name][1]]
        row_bias = sb("row_bias", [P, 6, D])
        self_mul = sb("self_mul", [P, S])
        self_add = sb("self_add", [P, S])
        
        x_dup = sb("x_dup", [P, 2, D])
        c_dup = sb("c_dup", [P, 2, D])
        res_a = sb("res_a", [P, D])
        stats_a = sb("stats_a", [P, 2, 6])
        mv_a = sb("mv_a", [P, 2, 2])
        small_a = sb("small_a", [P, 8, 2])
        x_hi = sb("x_hi", [P, 2, D], F32R)
        x_lo = sb("x_lo", [P, 2, D], F32R)
        c_hi = sb("c_hi", [P, 2, D], F32R)
        c_lo = sb("c_lo", [P, 2, D], F32R)
        q_split = sb("q_split", [P, 2, 2, D], F32R)
        k_hi = sb("k_hi", [P, 2, 2, D], F32R)
        k_lo = sb("k_lo", [P, 2, 2, D], F32R)
        c_split = k_hi[:, 1, :, :]
        v_a = sb("v_a", [P, 2, KT, H0 * S])
        p_a = sb("p_a", [P, 2, KT, D])
        pt_a = sb("pt_a", [P, 2, KT, D])
        xn_a = pt_a[:, 0, :, :]
        max_a = sb("max_a", [P, 2, KT])
        nmax_a = sb("nmax_a", [P, 2, KT])
        sum_a = sb("sum_a", [P, 2, KT])
        rec_a = sb("rec_a", [P, 2, KT])
        x1 = sb("x1", [P, D])

        scores_bank = [bank("scores0"), bank("scores1")]
        transposed_bank = bank("transposed")
        project_bank = bank("project")
        attended_bank = bank("attended")

        A = {n: sem("a_" + n) for n in (
            "x_in",             "stats", "mv", "mean_ps", "mean", "dev", "sq", "var", "var_ps", "eps", "rstd", "scale", "shift", "bias",
            "norm", "xhi", "xlo", "chi", "clo", "csplit", "v_ps", "v_sb", "q_ps", "q_hi", "q_lo", "k_ps", "k_hi",
            "k_lo", "scores", "max", "nmax", "exp", "rec", "prob", "trans", "pt0", "pt1", "att", "res", "x1")}

        def stage(name, banks, fills, blocks, W):
            T = Stage()
            T.banks, T.fills, T.W = banks, {f: n for n, f in enumerate(fills)}, W
            t = lambda n, shape, dt=F32: sb(f"{name}_{n}", shape, dt)
            T.c = t("c", [P, D])
            T.stats, T.mv, T.eps, T.msq, T.rstd = t("stats", [P, 6]), t("mv", [P, 2]), t("eps", [P, 1]), t("msq", [P, 1]), t("rstd", [P, 1])
            T.xn = t("xn", [P, D])
            T.xnT = t("xnT", [P, KT, P])
            T.xT = t("xT", [P, blocks * KT, P])
            T.qT = t("qT", [P, KT, P])
            T.kT = t("kT", [P, blocks, KT, P])
            T.kblk = t("kblk", [P, KT, blocks, 2, HB, S])
            T.v = t("v", [P, blocks, 2, HEADS // 2, 2, HD])
            T.p = t("p", [P, KT, HB * blocks * S])
            T.pt = t("pt", [P, KT, blocks, HB // 2, P])
            T.max, T.sum, T.rec = t("max", [P, KT, HB]), t("sum", [P, KT, HB]), t("rec", [P, KT, HB])
            T.yT = t("yT", [P, KT, P])
            T.res = t("res", [P, D])
            T.mid = t("mid", [P, 2, D])
            T.hid = T.pt[:, :, :, :, :].rearrange("p f c g q -> p (f c g) q")[:, 0:MT, :]
            T.s = {n: sem(f"{name}_{n}") for n in (
                "stats", "mv", "eps", "msq", "rstd", "xn", "mask", "kblk", "madd", "max", "sub", "exp", "sum", "rec",
                "prob", "res", "hid")}
            T.full = [sem(f"{name}_full{i}") for i in range(len(banks))]
            T.free = [sem(f"{name}_free{i}") for i in range(len(banks))]
            return T

        B = stage("b", [bank("b_bank0")], FILLS_B, 2, WBt)
        B.x2T = sb("b_x2T", [P, KT, P])
        C = stage("c", [bank("c_bank0"), bank("c_bank1")], FILLS_C, 1, WCt)
        def views(scratch, table):
            got, at = [], 0
            for parts, a, b in table:
                got.append(scratch[0:parts, at:at + a * b].rearrange("p (a b) -> p a b", a=a))
                at += a * b
            return got

        rows, wq_raw, wk_raw, wo_raw = views(B.kblk[:, :, :, :, :, :].rearrange("p f c b h k -> p (f c b h k)"),
                                             ((P, len(ROWS), D), (P, H0, P), (P, H0, P), (S, H0, S)))
        wv_raw, spread = views(B.p[:, :, :].rearrange("p f k -> p (f k)"), ((S, H0, P), (P, 4 * KT, P)))
        spread = spread.rearrange("p (n k) q -> p n k q", k=KT)
        x3 = sb("x3", [P, D])
        y_out = sb("y_out", [P, D])
        m1_raw = sb("m1_raw", [P, S], U8)
        m2_raw = sb("m2_raw", [P, S], I32)
        m1 = sb("m1", [P, S])
        m2 = sb("m2", [P, S])
        m4_raw = sb("m4_raw", [P, S])
        m4_mul = sb("m4_mul", [P, S])
        m4_add = sb("m4_add", [P, S])
        loaded = sem("loaded")
        stored = sem("stored")
        setup = {n: sem("setup_" + n) for n in ("consts", "zeros", "raw", "weights", "fold_ps", "fold", "mid_ps", "mid", "step", "tanh", "scaled", "spread", "row_ps", "row")}
        clear = range(min(s.num for s in sems), max(s.num for s in sems) + 1)
        assert len(clear) == len(sems)

        def fill_bank(T, eng, name):
            n = T.fills[name]
            i, k = n % len(T.banks), n // len(T.banks)
            if k:
                eng.wait_ge(T.free[i], k)
            return T.banks[i]

        def filled(T, ins, name):
            ins.then_inc(T.full[T.fills[name] % len(T.banks)], 1)

        def wait_fill(T, eng, name):
            n = T.fills[name]
            eng.wait_ge(T.full[n % len(T.banks)], n // len(T.banks) + 1)
            return T.banks[n % len(T.banks)]

        def release(T, ins, name):
            ins.then_inc(T.free[T.fills[name] % len(T.banks)], 1)

        def bc(ap, axis, n):
            ap = ap.unsqueeze(axis)
            shape = list(ap.shape)
            shape[axis] = n
            return ap.to_broadcast(shape)

        mm = nc.tensor.matmul

        def load_a(sp, i):
            for dup in range(2):
                sp.dma_start(x_dup[dup * S:(dup + 1) * S, :, :], dram["x"][pair(i)].rearrange("n c s -> c n s")).then_inc(loaded, 16)
                sp.dma_start(c_dup[dup * S:(dup + 1) * S, :, :], dram["ctx"][pair(i)].rearrange("n c s -> c n s")).then_inc(loaded, 16)
            return 4 * 16

        def pair(i):
            return bass.ds(2 * i, 2)

        with nc.Block() as block:

            @block.sync
            def _(sp):
                n = 0
                for dst, src in ((cols[:, :], dram["cols"]), (wq_raw[:, :, :], dram["wq0"]), (wk_raw[:, :, :], dram["wk0"]),
                                 (wv_raw[:, :, :], dram["wv0"]), (wo_raw[:, :, :], dram["wo0"]), (bv_raw[:, :], dram["bv0"])):
                    sp.dma_start(dst, src).then_inc(loaded, 16)
                    n += 16
                n += load_a(sp, 0)
                sp.wait_ge(loaded, n)
                sp.sem_inc(setup["raw"], 1)

            @block.gpsimd
            def _(pool):
                pool.memset(ident[:, :], 0.0).then_inc(setup["zeros"], 1)
                pool.memset(head_mask[:, :], 1.0).then_inc(setup["zeros"], 1)
                pool.memset(mean_of_all[:, :], 1.0 / P).then_inc(setup["consts"], 1)
                pool.memset(minus_half[:, :], -0.5).then_inc(setup["consts"], 1)
                pool.memset(B.v[:, :, :, :, :, :], 0.0).then_inc(setup["consts"], 1)
                pool.memset(C.v[:, :, :, :, :, :], 0.0).then_inc(setup["consts"], 1)
                pool.wait_ge(setup["zeros"], 2)
                pool.affine_select(out=ident[:, :], in_=ident[:, :], compare_op=ALU.not_equal, fill=1.0,
                                   base=0, pattern=[[-1, P]], channel_multiplier=1).then_inc(setup["consts"], 1)
                pool.affine_select(out=head_mask[:, :], in_=head_mask[:, :], compare_op=ALU.is_ge, fill=0.0,
                                   base=0, pattern=[[-HD, HB]], channel_multiplier=1).then_inc(setup["zeros"], 1)
                pool.wait_ge(setup["zeros"], 3)
                pool.affine_select(out=head_mask[:, :], in_=head_mask[:, :], compare_op=ALU.is_ge, fill=0.0,
                                   base=HD - 1, pattern=[[HD, HB]], channel_multiplier=-1).then_inc(setup["consts"], 1)

            @block.tensor
            def _(pe):
                pe.wait_ge(setup["raw"], 1)
                for h in range(H0):
                    last = mm(scores_bank[0][:, h * S:(h + 1) * S], wv_raw[:, h, :], wo_raw[:, h, :], start=True, stop=True)
                last.then_inc(setup["mid_ps"], 1)
                for h in range(H0):
                    for half in range(2):
                        last = mm(scores_bank[1][half * S:(half + 1) * S, 0:1], wo_raw[:, h, :], bv_raw[:, h:h + 1],
                                  start=h == 0, stop=h == H0 - 1)
                last.then_inc(setup["mid_ps"], 1)
            @block.vector
            def _(dve):
                dve.wait_ge(setup["raw"], 1)
                for n, (split, raw) in enumerate(((wq_split, wq_raw), (wk_split, wk_raw))):
                    dve.tensor_copy(split[:, :, :], raw[:, :, :]).then_inc(setup["step"], 1)
                    dve.wait_ge(setup["step"], n + 1)
                    dve.tensor_tensor(split[S:P, :, :], raw[S:P, :, :], split[S:P, :, :].bitcast(F32), ALU.subtract)
                dve.wait_ge(setup["mid_ps"], 2)
                dve.tensor_copy(wvo_hi[:, :], scores_bank[0][:, :]).then_inc(setup["step"], 1)
                dve.wait_ge(setup["step"], 3)
                dve.tensor_tensor(wvo_lo[:, :], scores_bank[0][:, :], wvo_hi[:, :].bitcast(F32), ALU.subtract)
                dve.tensor_tensor(out_bias0[:, :], scores_bank[1][:, 0:1], col("l0_bo"), ALU.add)

        def load_b(sp, i):
            sp.dma_start(B.c[:, :], dram["ctx"][pair(i)].rearrange("n c s -> (n c) s")).then_inc(loaded, 16)
            for b in range(2):
                sp.dma_start(m1_raw[b * S:(b + 1) * S, :], dram["mask1"][bass.ds(2 * i + b, 1), :].rearrange("o k -> (o k)").partition_broadcast(S)).then_inc(loaded, 16)
                sp.dma_start(m2_raw[b * S:(b + 1) * S, :], dram["mask2"][bass.ds(2 * i + b, 1), :].rearrange("o k -> (o k)").partition_broadcast(S)).then_inc(loaded, 16)
            return 5 * 16

        def load_c(sp, i):
            sp.dma_start(C.c[:, :], dram["ctx"][pair(i)].rearrange("n c s -> (n c) s")).then_inc(loaded, 16)
            sp.dma_start(m4_raw[:, :], dram["mask4"][pair(i)].rearrange("n q k -> (n q) k")).then_inc(loaded, 16)
            return 2 * 16

        nc.all_engine_barrier(sems_to_clear=clear)

        def head_step(h, k=0.0):
            return 8 + 4.75 * h + k

        def pe_a():
            yield 1
            pe = nc.tensor
            pe.wait_ge(A["mv"], 2)
            mm(project_bank[:, 0:2], mean_of_all[:, :], mv_a[:, :, 0], start=True, stop=True).then_inc(A["mean_ps"], 1)
            yield 3
            pe.wait_ge(A["var"], 1)
            mm(project_bank[:, 2:4], mean_of_all[:, :], small_a[:, 3, :], start=True, stop=True).then_inc(A["var_ps"], 1)
            yield 6
            pe.wait_ge(A["csplit"], 1)
            pe.wait_ge(A["eps"], 1)
            for n in range(2):
                for kt in range(KT):
                    if n or kt:
                        yield 6
                    ps = (*scores_bank, transposed_bank, project_bank)[2 * n + kt]
                    lhs = c_split[:, n, kt * P:(kt + 1) * P]
                    mm(ps[:, :], lhs, wvo_hi[:, :], start=True, stop=False)
                    mm(ps[:, :], lhs, wvo_lo[:, :], start=False, stop=True).then_inc(A["v_ps"], 1)
            def project(h):
                if h == 0:
                    pe.wait_ge(A["v_sb"], 4)
                    pe.wait_ge(A["xlo"], 1)
                else:
                    pe.wait_ge(A["k_lo"], h)
                mm(project_bank[:, :], wq_split[:, h, :], x_hi[:, :, :], start=True, stop=False)
                mm(project_bank[:, :], wq_split[:, h, :], x_lo[:, :, :], start=False, stop=True).then_inc(A["q_ps"], 1)

            def project_keys(h):
                pe.wait_ge(A["q_lo"], h + 1)
                mm(project_bank[:, :], wk_split[:, h, :], c_hi[:, :, :], start=True, stop=False)
                mm(project_bank[:, :], wk_split[:, h, :], c_lo[:, :, :], start=False, stop=True).then_inc(A["k_ps"], 1)

            def score(h, n):
                pe.wait_ge(A["k_lo"], h + 1)
                if h:
                    pe.wait_ge(A["exp"], 2 * h - 1 + n)
                for qt in range(KT):
                    lhs = q_split[:, h % 2, n, qt * P:(qt + 1) * P]
                    ps = scores_bank[n][:, qt * D:(qt + 1) * D]
                    mm(ps, lhs, k_hi[:, h % 2, n, :], start=True, stop=False)
                    last = mm(ps, lhs, k_lo[:, h % 2, n, :], start=False, stop=True)
                last.then_inc(A["scores"], 1)

            def transpose(h, n):
                pe.wait_ge(A["prob"], 2 * h + n + 1)
                if n:
                    pe.wait_ge(A["pt0"], h + 1)
                elif h:
                    pe.wait_ge(A["pt1"], h)
                for qt in range(KT):
                    for kt in range(KT):
                        last = nc.tensor.transpose(transposed_bank[:, kt * D + qt * P:kt * D + (qt + 1) * P],
                                                   p_a[:, n, qt, kt * P:(kt + 1) * P], ident[:, :])
                last.then_inc(A["trans"], 1)

            def attend(h):
                pe.wait_ge(A["pt0"], h + 1)
                pe.wait_ge(A["pt1"], h + 1)
                for kt in range(KT):
                    for n in range(2):
                        last = mm(attended_bank[n * S:(n + 1) * S, 0:D], v_a[:, n, kt, h * S:(h + 1) * S], pt_a[:, n, kt, :],
                                  start=h == 0 and kt == 0, stop=h == H0 - 1 and kt == KT - 1)
                last.then_inc(A["att"], 1)

            yield head_step(0)
            project(0)
            yield head_step(0, 0.5)
            project_keys(0)
            yield head_step(0, 1)
            score(0, 0)
            yield head_step(0, 1)
            score(0, 1)
            yield head_step(0, 1.2)
            project(1)
            yield head_step(0, 1.5)
            project_keys(1)
            for h in range(H0):
                if h + 1 < H0:
                    for n in range(2):
                        yield head_step(h, 3 + 0.2 * n)
                        score(h + 1, n)
                yield head_step(h, 3.5)
                transpose(h, 0)
                if h + 2 < H0:
                    yield head_step(h, 3.8)
                    project(h + 2)
                yield head_step(h, 4)
                transpose(h, 1)
                if h + 2 < H0:
                    yield head_step(h, 4.6)
                    project_keys(h + 2)
                yield head_step(h, 5.25)
                attend(h)

        def dve_a(b_runs):
            dve = nc.vector
            yield 0
            for n in range(2):
                dve.bn_stats(stats_a[:, n, :], x_dup[:, n, :]).then_inc(A["stats"], 1)
            dve.wait_ge(A["stats"], 2)
            for n in range(2):
                dve.bn_aggr(mv_a[:, n, :], stats_a[:, n, :]).then_inc(A["mv"], 1)
            yield 2
            mean, dev, sq, var, eps, scale, shift, bias = (small_a[:, j, :] for j in range(8))
            dve.wait_ge(A["mean_ps"], 1)
            dve.tensor_copy(mean, project_bank[:, 0:2]).then_inc(A["mean"], 1)
            dve.wait_ge(A["mean"], 1)
            dve.tensor_tensor(dev, mv_a[:, :, 0], mean, ALU.subtract).then_inc(A["dev"], 1)
            dve.wait_ge(A["dev"], 1)
            dve.tensor_tensor(sq, dev, dev, ALU.mult).then_inc(A["sq"], 1)
            dve.wait_ge(A["sq"], 1)
            dve.tensor_tensor(var, sq, mv_a[:, :, 1], ALU.add).then_inc(A["var"], 1)
            yield 4
            dve.wait_ge(A["chi"], 1)
            dve.tensor_tensor(c_lo[:, :, :], c_dup[:, :, :], c_hi[:, :, :].bitcast(F32), ALU.subtract).then_inc(A["clo"], 1)
            dve.tensor_copy(c_split[0:S, :, :], c_dup[0:S, :, :])
            dve.tensor_tensor(c_split[S:P, :, :], c_dup[S:P, :, :], c_hi[S:P, :, :].bitcast(F32), ALU.subtract).then_inc(A["csplit"], 1)
            yield 4.2
            dve.wait_ge(A["var_ps"], 1)
            dve.tensor_scalar(eps, project_bank[:, 2:4], 1e-5, None, ALU.add).then_inc(A["eps"], 1)
            yield 5
            dve.wait_ge(A["rstd"], 1)
            dve.tensor_scalar(scale, bias, col("l0_gamma"), None, ALU.mult).then_inc(A["scale"], 1)
            dve.wait_ge(A["scale"], 1)
            dve.tensor_tensor(shift, mean, scale, ALU.mult).then_inc(A["shift"], 1)
            dve.wait_ge(A["shift"], 1)
            dve.tensor_scalar(bias, shift, -1.0, col("l0_beta"), ALU.mult, ALU.add).then_inc(A["bias"], 1)
            dve.wait_ge(A["bias"], 1)
            for n in range(2):
                dve.tensor_scalar(xn_a[:, n, :], x_dup[:, n, :], scale[:, n:n + 1], bias[:, n:n + 1], ALU.mult, ALU.add).then_inc(A["norm"], 1)
            yield 7
            dve.wait_ge(A["xhi"], 1)
            dve.tensor_tensor(x_lo[:, :, :], xn_a, x_hi[:, :, :].bitcast(F32), ALU.subtract).then_inc(A["xlo"], 1)

            def low_queries(h):
                dve.wait_ge(A["q_hi"], h + 1)
                dve.scalar_tensor_tensor(q_split[S:P, h % 2, :, :], project_bank[S:P, :], col("l0_bq")[S:P, h:h + 1],
                                         q_split[S:P, h % 2, :, :].bitcast(F32), ALU.add, ALU.subtract).then_inc(A["q_lo"], 1)

            def low_keys(h):
                dve.wait_ge(A["k_hi"], h + 1)
                if h > 1:
                    dve.wait_ge(A["scores"], 2 * (h - 1))
                dve.scalar_tensor_tensor(k_lo[:, h % 2, :, :], project_bank[:, :], col("l0_bk")[:, h:h + 1],
                                         k_hi[:, h % 2, :, :].bitcast(F32), ALU.add, ALU.subtract).then_inc(A["k_lo"], 1)

            def maxima(h, n):
                dve.wait_ge(A["scores"], 2 * h + n + 1)
                dve.tensor_reduce(max_a[:, n, :], scores_bank[n][:, :].rearrange("p (q k) -> p q k", q=KT), AX.X, ALU.max).then_inc(A["max"], 1)
                dve.wait_ge(A["max"], 2 * h + n + 1)
                if h:
                    dve.wait_ge(A["exp"], 2 * h - 1 + n)
                dve.tensor_scalar(nmax_a[:, n, :], max_a[:, n, :], -(S ** -0.5), None, ALU.mult).then_inc(A["nmax"], 1)

            yield head_step(0, 0.25)
            low_queries(0)
            yield head_step(0, 0.75)
            low_keys(0)
            yield head_step(0, 1.25)
            maxima(0, 0)
            yield head_step(0, 1.25)
            maxima(0, 1)
            yield head_step(0, 1.4)
            low_queries(1)
            yield head_step(0, 1.8)
            low_keys(1)
            for h in range(H0):
                for n in range(2):
                    yield head_step(h, 2)
                    dve.wait_ge(A["exp"], 2 * h + n + 1)
                    dve.reciprocal(rec_a[:, n, :], sum_a[:, n, :]).then_inc(A["rec"], 1)
                if h + 1 < H0:
                    for n in range(2):
                        yield head_step(h, 3.2 + 0.2 * n)
                        maxima(h + 1, n)
                if h + 2 < H0:
                    yield head_step(h, 4)
                    low_queries(h + 2)
                yield head_step(h, 4.5)
                dve.wait_ge(A["trans"], 2 * h + 2)
                if h:
                    dve.wait_ge(A["att"], h)
                dve.tensor_copy(pt_a[:, 1, :, :], transposed_bank[:, :].rearrange("p (k q) -> p k q", k=KT)).then_inc(A["pt1"], 1)
                if h + 2 < H0:
                    yield head_step(h, 5)
                    low_keys(h + 2)
            yield head_step(H0, 2)
            dve.wait_ge(A["att"], H0)
            dve.wait_ge(A["res"], 1)
            if b_runs:
                dve.wait_ge(B.full[0], 1)
                dve.wait_ge(B.s["res"], 1)
            dve.tensor_tensor(x1[:, :], attended_bank[:, 0:D], res_a[:, :], ALU.add).then_inc(A["x1"], 1)

        def act_a():
            act = nc.scalar
            yield 0
            act.activation(c_hi[:, :, :], c_dup[:, :, :], ACT.Copy).then_inc(A["chi"], 1)
            yield 6
            act.wait_ge(A["norm"], 2)
            act.activation(x_hi[:, :, :], xn_a, ACT.Copy).then_inc(A["xhi"], 1)
            for n in range(2):
                for kt in range(KT):
                    yield 6.2
                    act.wait_ge(A["v_ps"], 2 * n + kt + 1)
                    act.activation(v_a[:, n, kt, :], (*scores_bank, transposed_bank, project_bank)[2 * n + kt][:, :], ACT.Copy).then_inc(A["v_sb"], 1)

            def high_queries(h):
                act.wait_ge(A["q_ps"], h + 1)
                if h > 1:
                    act.wait_ge(A["scores"], 2 * (h - 1))
                act.activation(q_split[:, h % 2, :, :], project_bank[:, :].rearrange("p (n s) -> p n s", n=2), ACT.Identity,
                               bias=col("l0_bq")[:, h:h + 1]).then_inc(A["q_hi"], 1)

            def high_keys(h):
                act.wait_ge(A["k_ps"], h + 1)
                if h > 1:
                    act.wait_ge(A["scores"], 2 * (h - 1))
                act.activation(k_hi[:, h % 2, :, :], project_bank[:, :].rearrange("p (n s) -> p n s", n=2), ACT.Identity,
                               bias=col("l0_bk")[:, h:h + 1]).then_inc(A["k_hi"], 1)

            def exponentials(h, n):
                act.wait_ge(A["nmax"], 2 * h + n + 1)
                if h:
                    act.wait_ge(A["trans"], 2 * h - 1 + n)
                    act.wait_ge(A["rec"], 2 * h - 1 + n)
                for qt in range(KT):
                    last = act.activation(p_a[:, n, qt, :], scores_bank[n][:, qt * D:(qt + 1) * D], ACT.Exp, scale=S ** -0.5,
                                          bias=nmax_a[:, n, qt:qt + 1], accum_out=sum_a[:, n, qt:qt + 1])
                last.then_inc(A["exp"], 1)

            yield head_step(0, 0.25)
            high_queries(0)
            yield head_step(0, 0.75)
            high_keys(0)
            yield head_step(0, 1.3)
            high_queries(1)
            yield head_step(0, 1.5)
            exponentials(0, 0)
            yield head_step(0, 1.5)
            exponentials(0, 1)
            yield head_step(0, 1.7)
            high_keys(1)
            for h in range(H0):
                yield head_step(h, 3.75)
                act.wait_ge(A["trans"], 2 * h + 1)
                if h:
                    act.wait_ge(A["att"], h)
                act.activation(pt_a[:, 0, :, :], transposed_bank[:, :].rearrange("p (k q) -> p k q", k=KT), ACT.Copy).then_inc(A["pt0"], 1)
                if h + 2 < H0:
                    yield head_step(h, 3.9)
                    high_queries(h + 2)
                if h + 1 < H0:
                    for n in range(2):
                        yield head_step(h, 4.1 + 0.4 * n)
                        exponentials(h + 1, n)
                if h + 2 < H0:
                    yield head_step(h, 4.8)
                    high_keys(h + 2)

        def pool_a():
            pool = nc.gpsimd
            yield 0
            pool.wait_ge(A["x_in"], 16)
            pool.tensor_scalar(res_a[:, :], res_a[:, :], out_bias0[:, :], 1.0, ALU.add, ALU.mult).then_inc(A["res"], 1)
            yield 4.5
            pool.wait_ge(A["eps"], 1)
            pool.tensor_tensor(small_a[:, 7, :], small_a[:, 4, :], minus_half[:, :], ALU.pow).then_inc(A["rstd"], 1)
            for h in range(H0):
                for n in range(2):
                    yield head_step(h, 2.25)
                    pool.wait_ge(A["rec"], 2 * h + n + 1)
                    for qt in range(KT):
                        last = pool.tensor_scalar(p_a[:, n, qt, :], p_a[:, n, qt, :], rec_a[:, n, qt:qt + 1], 1.0, ALU.mult, ALU.mult)
                    last.then_inc(A["prob"], 1)

        ATT = 11

        def unit(T, a, f, c, blocks):
            before = (T.blocks[0] * KT) if a else 0
            return before + f * blocks + c + 1

        B.blocks, C.blocks = (1, 2), (1, 1)

        def pe_transposes(T, name, srcs):
            ps = fill_bank(T, nc.tensor, name)
            n = 0
            for src in srcs:
                for k in range(KT):
                    last = nc.tensor.transpose(ps[:, n * P:(n + 1) * P], src[:, k * P:(k + 1) * P], ident[:, :])
                    n += 1
            filled(T, last, name)

        def pe_project_T(T, name, w, srcT):
            ps = fill_bank(T, nc.tensor, name)
            for m in range(KT):
                for k in range(KT):
                    last = mm(ps[:, m * P:(m + 1) * P], w[:, k, m * P:(m + 1) * P], srcT[:, k, :], start=k == 0, stop=k == KT - 1)
            filled(T, last, name)

        def pe_values(T, name, w, srcT):
            ps = fill_bank(T, nc.tensor, name)
            wv = w.rearrange("p k (g e d) -> p k g e d", e=2, d=HD)
            for b in range(2):
                for k in range(KT):
                    for e in range(2):
                        last = mm(ps[e * S:(e + 1) * S, b * P:(b + 1) * P], srcT[:, k, b * S:(b + 1) * S], wv[:, k, :, e, :],
                                  start=k == 0, stop=k == KT - 1)
            filled(T, last, name)

        def written(T, eng, name):
            n = T.fills[name]
            eng.wait_ge(T.free[n % len(T.banks)], n // len(T.banks) + 1)

        def pe_attention(T, a, base):
            pe, blocks = nc.tensor, T.blocks[a]
            for f in range(KT):
                for c in range(blocks):
                    yield base + 1 + f + 0.5 * c
                    written(T, pe, (a, "q"))
                    pe.wait_ge(T.s["kblk"], unit(T, a, f, c, blocks))
                    ps = fill_bank(T, pe, (a, "s", f, c))
                    for b in range(2):
                        last = mm(ps[b * S:(b + 1) * S, :], T.qT[:, f, b * S:(b + 1) * S], T.kblk[:, f, c, b, :, :], start=True, stop=True)
                    filled(T, last, (a, "s", f, c))
            for f in range(KT):
                p = T.p[:, f, 0:HB * blocks * S].rearrange("p (c m) -> p c m", c=blocks)
                for c in range(blocks):
                    yield base + 6 + 1.5 * f + 0.5 * c
                    pe.wait_ge(T.s["prob"], 2 * a + f + 1)
                    ps = fill_bank(T, pe, (a, "t", f, c))
                    for g in range(HB // 2):
                        last = nc.tensor.transpose(ps[:, g * P:(g + 1) * P], p[:, c, g * P:(g + 1) * P], ident[:, :])
                    filled(T, last, (a, "t", f, c))
                yield base + 7.4 + 1.5 * f
                for c in range(blocks):
                    written(T, pe, (a, "v", c))
                    written(T, pe, (a, "t", f, c))
                ps = fill_bank(T, pe, (a, "o", f))
                for b in range(2):
                    for c in range(blocks):
                        for g in range(HB // 2):
                            last = mm(ps[32 * g:32 * (g + 1), b * S:(b + 1) * S], T.v[:, c, b, f * (HB // 2) + g, :, :],
                                      T.pt[:, f, c, g, b * S:(b + 1) * S], start=c == 0, stop=c == blocks - 1)
                filled(T, last, (a, "o", f))
            yield base + 10
            for f in range(KT):
                written(T, pe, (a, "o", f))
            ps = fill_bank(T, pe, (a, "p"))
            for f in range(KT):
                last = mm(ps[:, 0:D], T.yT[:, f, :], T.W[f"o{a}"][:, f, :], start=f == 0, stop=f == KT - 1)
            filled(T, last, (a, "p"))

        def dve_attention(T, a, base, masked):
            dve, blocks = nc.vector, T.blocks[a]

            def view(f):
                return T.p[:, f, 0:HB * blocks * S].rearrange("p (c h k) -> p c h k", c=blocks, h=HB)

            def per_head(ap):
                return bc(bc(ap, 2, S), 1, blocks)

            def whole_rows(f):
                return view(f).rearrange("p c h k -> p h c k")

            for f in range(KT):
                i = 2 * a + f + 1
                for c in range(blocks):
                    yield base + 1.5 + f + 0.5 * c
                    ps = wait_fill(T, dve, (a, "s", f, c))
                    ins = masked(c, ps[:, :].rearrange("p (h k) -> p h k", h=HB), view(f)[:, c, :, :])
                    release(T, ins, (a, "s", f, c))
                yield base + 2.4 + f
                if T is C:
                    dve.wait_ge(T.s["madd"], i)
                else:
                    for c in range(blocks):
                        written(T, dve, (a, "s", f, c))
                dve.tensor_reduce(T.max[:, f, :], whole_rows(f), AX.XY, ALU.max).then_inc(T.s["max"], 1)
                dve.wait_ge(T.s["max"], i)
                dve.tensor_tensor(view(f), view(f), per_head(T.max[:, f, :]), ALU.subtract).then_inc(T.s["sub"], 1)
            for f in range(KT):
                i = 2 * a + f + 1
                yield base + 4.5 + f
                dve.wait_ge(T.s["exp"], i)
                dve.tensor_reduce(T.sum[:, f, :], whole_rows(f), AX.XY, ALU.add).then_inc(T.s["sum"], 1)
                dve.wait_ge(T.s["sum"], i)
                dve.reciprocal(T.rec[:, f, :], T.sum[:, f, :]).then_inc(T.s["rec"], 1)
            yield base + 10.5
            ps = wait_fill(T, dve, (a, "p"))
            dve.wait_ge(T.s["res"], a + 1)
            ins = dve.tensor_tensor(T.mid[:, a, :], ps[:, 0:D], T.res[:, :], ALU.add)
            release(T, ins, (a, "p"))

        def act_attention(T, a, base):
            act, blocks = nc.scalar, T.blocks[a]
            for f in range(KT):
                yield base + 3.5 + f
                p = T.p[:, f, 0:HB * blocks * S]
                act.wait_ge(T.s["sub"], 2 * a + f + 1)
                act.activation(p, p, ACT.Exp).then_inc(T.s["exp"], 1)
            for f in range(KT):
                for c in range(blocks):
                    yield base + 6.4 + 1.5 * f + 0.5 * c
                    ps = wait_fill(T, act, (a, "t", f, c))
                    ins = act.activation(T.pt[:, f, c, :, :], ps[:, :].rearrange("p (g q) -> p g q", q=P), ACT.Copy)
                    release(T, ins, (a, "t", f, c))
                yield base + 7.8 + 1.5 * f
                ps = wait_fill(T, act, (a, "o", f))
                release(T, act.activation(T.yT[:, f, :], ps[:, 0:P], ACT.Copy), (a, "o", f))

        def pool_keys(T, a, c, base, f):
            pool, blocks = nc.gpsimd, T.blocks[a]
            yield base
            written(T, pool, (a, "k", c))
            if a:
                written(T, pool, (0, "p"))
            for b in range(2):
                last = pool.tensor_tensor(T.kblk[:, f, c, b, :, :], bc(T.kT[:, c, f, b * S:(b + 1) * S], 1, HB), bc(head_mask[:, :], 2, S), ALU.mult)
            last.then_inc(T.s["kblk"], 1)

        def pool_attention(T, a, base, mask_add):
            pool, blocks = nc.gpsimd, T.blocks[a]
            for f in range(KT):
                for c in range(blocks):
                    yield from pool_keys(T, a, c, base + 0.3 * f, f)
            for f in range(KT):
                if mask_add is not None:
                    yield base + 2 + f
                    written(T, pool, (a, "s", f, 0))
                    v = T.p[:, f, 0:HB * S].rearrange("p (h k) -> p h k", h=HB)
                    pool.tensor_tensor(v, v, bc(mask_add[:, :], 1, HB), ALU.add).then_inc(T.s["madd"], 1)
            for f in range(KT):
                yield base + 5 + f
                pool.wait_ge(T.s["rec"], 2 * a + f + 1)
                v = T.p[:, f, 0:HB * blocks * S].rearrange("p (c h k) -> p c h k", c=blocks, h=HB)
                pool.tensor_tensor(v, v, bc(bc(T.rec[:, f, :], 2, S), 1, blocks), ALU.mult).then_inc(T.s["prob"], 1)

        def pool_residual(T, n, step, src, row, ready):
            yield step
            ready(nc.gpsimd)
            nc.gpsimd.tensor_tensor(T.res[:, :], src, row_bias[:, row, :], ALU.add).then_inc(T.s["res"], 1)

        def dve_norm(T, n, step, src, eps, rms=False):
            dve = nc.vector
            yield step
            dve.bn_stats(T.stats[:, :], src).then_inc(T.s["stats"], 1)
            dve.wait_ge(T.s["stats"], n + 1)
            dve.bn_aggr(T.mv[:, :], T.stats[:, :]).then_inc(T.s["mv"], 1)
            dve.wait_ge(T.s["mv"], n + 1)
            mean, var = T.mv[:, 0:1], T.mv[:, 1:2]
            if rms:
                dve.scalar_tensor_tensor(T.msq[:, :], mean, mean, var, ALU.mult, ALU.add).then_inc(T.s["msq"], 1)
                dve.wait_ge(T.s["msq"], 1)
                var = T.msq[:, :]
            dve.tensor_scalar(T.eps[:, :], var, eps, None, ALU.add).then_inc(T.s["eps"], 1)
            yield step + 2
            dve.wait_ge(T.s["rstd"], n + 1)
            if n:
                written(T, dve, f"nT{n - 1}")
            if rms:
                dve.tensor_scalar(T.xn[:, :], src, T.rstd[:, :], 1.0, ALU.mult, ALU.mult).then_inc(T.s["xn"], 1)
            else:
                dve.tensor_scalar(T.xn[:, :], src, mean, T.rstd[:, :], ALU.subtract, ALU.mult).then_inc(T.s["xn"], 1)

        def pool_norm(T, n, step):
            yield step + 1
            nc.gpsimd.wait_ge(T.s["eps"], n + 1)
            nc.gpsimd.tensor_tensor(T.rstd[:, :], T.eps[:, :], minus_half[:, 0:1], ALU.pow).then_inc(T.s["rstd"], 1)

        def pe_norm(T, n, step):
            yield step + 2.5
            nc.tensor.wait_ge(T.s["xn"], n + 1)
            pe_transposes(T, f"nT{n}", [T.xn])

        def act_copy(T, step, name, dst, width):
            yield step
            ps = wait_fill(T, nc.scalar, name)
            release(T, nc.scalar.activation(dst, ps[:, 0:width], ACT.Copy), name)

        def act_norm(T, n, step):
            yield from act_copy(T, step + 3, f"nT{n}", T.xnT[:, :, :], D)

        def act_values(T, a, c, step):
            yield step
            ps = wait_fill(T, nc.scalar, (a, "v", c))
            for e in range(2):
                last = nc.scalar.activation(T.v[e * S:(e + 1) * S, c, :, :, e, :],
                                            ps[e * S:(e + 1) * S, 0:D].rearrange("p (b g d) -> p b g d", b=2, d=HD), ACT.Copy)
            release(T, last, (a, "v", c))

        def dve_bias(T, step, name, dst, bias):
            yield step
            ps = wait_fill(T, nc.vector, name)
            n = bias.shape[1]
            ins = nc.vector.tensor_tensor(dst, ps[:, 0:n * P].rearrange("p (m t) -> p m t", t=P), bc(bias, 2, P), ALU.add)
            release(T, ins, name)

        def pe_mlp(T, n, step):
            pe = nc.tensor
            for half in range(2):
                yield step + 1.5 * half
                written(T, pe, f"nT{n}")
                ps = fill_bank(T, pe, f"h{half}")
                for m in range(MT // 2):
                    cols_ = slice((half * MT // 2 + m) * P, (half * MT // 2 + m + 1) * P)
                    for k in range(KT):
                        last = mm(ps[:, m * P:(m + 1) * P], T.W["w1"][:, k, cols_], T.xnT[:, k, :], start=k == 0, stop=k == KT - 1)
                filled(T, last, f"h{half}")
            for m in range(MT):
                if m % (MT // 2) == 0:
                    yield step + 4 + 1.5 * (m > 0)
                    pe.wait_ge(T.s["hid"], 2 * m // MT + 1)
                    if m == 0:
                        ps = fill_bank(T, pe, "y")
                last = mm(ps[:, 0:D], T.hid[:, m, :], T.W["w2"][:, m, :], start=m == 0, stop=m == MT - 1)
            filled(T, last, "y")

        def dve_mlp(T, step, bias, dst, ready):
            for half in range(2):
                m = half * MT // 2
                yield from dve_bias(T, step + 0.7 + 1.5 * half, f"h{half}", T.hid[:, m:m + MT // 2, :], bias[:, m:m + MT // 2])
            yield step + 6
            ps = wait_fill(T, nc.vector, "y")
            nc.vector.wait_ge(T.s["res"], 3)
            ready(nc.vector)
            release(T, nc.vector.tensor_tensor(dst, ps[:, 0:D], T.res[:, :], ALU.add), "y")

        def act_mlp(T, step):
            for half in range(2):
                yield step + 1 + 1.5 * half
                written(T, nc.scalar, f"h{half}")
                h = T.hid[:, half * MT // 2:(half + 1) * MT // 2, :]
                nc.scalar.activation(h, h, ACT.Gelu_apprx_tanh).then_inc(T.s["hid"], 1)

        def pe_b():
            pe = nc.tensor
            yield 0
            pe_transposes(B, "xT", [B.c, x1])
            yield from pe_norm(B, 0, 0)
            yield 3.5
            written(B, pe, "xT")
            pe_project_T(B, (0, "q"), B.W["q0"], B.xT[:, KT:2 * KT, :])
            yield 4
            written(B, pe, "nT0")
            pe_project_T(B, (0, "k", 0), B.W["k0"], B.xnT)
            yield 4.5
            pe_values(B, (0, "v", 0), B.W["v0"], B.xnT)
            yield from pe_attention(B, 0, 5)
            yield 16
            written(B, pe, (0, "p"))
            pe_transposes(B, "x2T", [B.mid[:, 0, :]])
            yield 17
            written(B, pe, "x2T")
            srcs = (B.xT[:, 0:KT, :], B.x2T)
            pe_project_T(B, (1, "q"), B.W["q1"], B.x2T)
            for c in range(2):
                yield 17.5 + 0.5 * c
                pe_project_T(B, (1, "k", c), B.W["k1"], srcs[c])
            for c in range(2):
                yield 18.5 + 0.5 * c
                pe_values(B, (1, "v", c), B.W["v1"], srcs[c])
            yield from pe_attention(B, 1, 19)
            yield from pe_norm(B, 1, 30)
            yield from pe_mlp(B, 1, 34)

        def dve_b(c_runs):
            dve = nc.vector
            yield from dve_norm(B, 0, 0, B.c[:, :], 1e-5)
            yield 3
            dve.tensor_scalar(m1[:, :], m1_raw[:, :], 0.0, NEG, ALU.is_equal, ALU.mult).then_inc(B.s["mask"], 1)
            dve.tensor_scalar(m2[:, :], m2_raw[:, :], 0.0, NEG, ALU.is_equal, ALU.mult).then_inc(B.s["mask"], 1)
            yield from dve_bias(B, 4.3, (0, "k", 0), B.kT[:, 0, :, :], fcol("bk1"))
            dve.wait_ge(B.s["mask"], 2)

            def masked(scale, mask):
                def run(c, ps, dst):
                    if mask is not None and c == 0:
                        return dve.scalar_tensor_tensor(dst, ps, scale, bc(mask[:, :], 1, HB), ALU.mult, ALU.add)
                    return dve.tensor_scalar(dst, ps, scale, None, ALU.mult)
                return run

            yield from dve_attention(B, 0, 5, masked(HD ** -0.5, m1))
            yield from dve_bias(B, 17.3, (1, "q"), B.qT[:, :, :], col("l2_bq"))
            for c in range(2):
                yield from dve_bias(B, 17.8 + 0.5 * c, (1, "k", c), B.kT[:, c, :, :], col("l2_bk"))
            yield from dve_attention(B, 1, 19, masked(1.0 / HD, m2))
            written(B, dve, (1, "p"))
            yield from dve_norm(B, 1, 30, B.mid[:, 1, :], 1e-6, rms=True)

            def x3_free(eng):
                if c_runs:
                    eng.wait_ge(C.s["xn"], 1)
                    eng.wait_ge(C.s["res"], 1)
            yield from dve_mlp(B, 34, col("l2_b1"), x3[:, :], x3_free)

        def act_b():
            yield from act_copy(B, 1, "xT", B.xT[:, :, :], 2 * D)
            yield from act_norm(B, 0, 0)
            yield from act_copy(B, 3.8, (0, "q"), B.qT[:, :, :], D)
            yield from act_values(B, 0, 0, 4.8)
            yield from act_attention(B, 0, 5)
            yield from act_copy(B, 16.5, "x2T", B.x2T[:, :, :], D)
            for c in range(2):
                yield from act_values(B, 1, c, 18.8 + 0.5 * c)
            yield from act_attention(B, 1, 19)
            yield from act_norm(B, 1, 30)
            yield from act_mlp(B, 34)

        def pool_b():
            yield from pool_residual(B, 0, 0, x1[:, :], 0, lambda pool: None)
            yield from pool_norm(B, 0, 0)
            yield from pool_attention(B, 0, 5, None)
            yield from pool_residual(B, 1, 16.5, B.mid[:, 0, :], 1, lambda pool: written(B, pool, (0, "p")))
            yield from pool_attention(B, 1, 19, None)
            yield from pool_norm(B, 1, 30)
            yield from pool_residual(B, 2, 31.5, B.mid[:, 0, :], 2, lambda pool: written(B, pool, (1, "p")))

        def pe_c():
            pe = nc.tensor
            yield 0
            pe_transposes(C, "xT", [C.c])
            yield from pe_norm(C, 0, 0)
            yield 3.5
            written(C, pe, "nT0")
            pe_project_T(C, (0, "q"), C.W["q0"], C.xnT)
            yield 4
            pe_project_T(C, (0, "k", 0), C.W["k0"], C.xnT)
            yield 4.5
            pe_values(C, (0, "v", 0), C.W["v0"], C.xnT)
            yield from pe_attention(C, 0, 5)
            yield from pe_norm(C, 1, 16)
            yield 19.5
            written(C, pe, "nT1")
            pe_project_T(C, (1, "q"), C.W["q1"], C.xnT)
            yield 20
            written(C, pe, "xT")
            pe_project_T(C, (1, "k", 0), C.W["k1"], C.xT)
            yield 20.5
            pe_values(C, (1, "v", 0), C.W["v1"], C.xT)
            yield from pe_attention(C, 1, 21)
            yield from pe_norm(C, 2, 32)
            yield from pe_mlp(C, 2, 36)

        def dve_c():
            dve = nc.vector
            yield from dve_norm(C, 0, 0, x3[:, :], 1e-5)
            yield 3
            dve.tensor_scalar(m4_mul[:, :], m4_raw[:, :], HD ** -0.5, None, ALU.mult).then_inc(C.s["mask"], 1)
            dve.tensor_scalar(m4_add[:, :], m4_raw[:, :], 10000.0, -10000.0, ALU.mult, ALU.add).then_inc(C.s["mask"], 1)
            yield from dve_bias(C, 3.8, (0, "q"), C.qT[:, :, :], fcol("q3"))
            yield from dve_bias(C, 4.3, (0, "k", 0), C.kT[:, 0, :, :], fcol("k3"))
            dve.wait_ge(C.s["mask"], 2)

            def masked(mask):
                return lambda c, ps, dst: dve.tensor_tensor(dst, ps, bc(mask[:, :], 1, HB), ALU.mult)

            yield from dve_attention(C, 0, 5, masked(self_mul))
            written(C, dve, (0, "p"))
            yield from dve_norm(C, 1, 16, C.mid[:, 0, :], 1e-5)
            yield from dve_bias(C, 19.8, (1, "q"), C.qT[:, :, :], fcol("q4"))
            yield from dve_bias(C, 20.3, (1, "k", 0), C.kT[:, 0, :, :], col("l3_bk"))
            yield from dve_attention(C, 1, 21, masked(m4_mul))
            written(C, dve, (1, "p"))
            yield from dve_norm(C, 2, 32, C.mid[:, 1, :], 1e-5)
            yield from dve_mlp(C, 36, fcol("b1"), y_out[:, :], lambda eng: eng.wait_ge(stored, 16))

        def act_c():
            yield from act_copy(C, 1, "xT", C.xT[:, 0:KT, :], D)
            yield from act_norm(C, 0, 0)
            yield from act_values(C, 0, 0, 4.8)
            yield from act_attention(C, 0, 5)
            yield from act_norm(C, 1, 16)
            yield from act_values(C, 1, 0, 20.8)
            yield from act_attention(C, 1, 21)
            yield from act_norm(C, 2, 32)
            yield from act_mlp(C, 36)

        def pool_c():
            yield from pool_residual(C, 0, 0, x3[:, :], 3, lambda pool: None)
            yield from pool_norm(C, 0, 0)
            yield from pool_attention(C, 0, 5, self_add)
            yield from pool_residual(C, 1, 16.5, C.mid[:, 0, :], 4, lambda pool: written(C, pool, (0, "p")))
            yield from pool_norm(C, 1, 16)
            yield 20
            nc.gpsimd.wait_ge(C.s["mask"], 2)
            yield from pool_attention(C, 1, 21, m4_add)
            yield from pool_residual(C, 2, 32.5, C.mid[:, 1, :], 5, lambda pool: written(C, pool, (1, "p")))
            yield from pool_norm(C, 2, 32)

        def load_s(sp):
            for dst, src in ((wb[:, :], dram["wb"]), (wc[:, :], dram["wc"]), (rows[:, :, :], dram["rows"].partition_broadcast(P)),
                             (gate[:, :], dram["gate"].partition_broadcast(P)),
                             (self_mul[0:S, :], dram["self_mask"]), (self_mul[S:P, :], dram["self_mask"])):
                sp.dma_start(dst, src).then_inc(setup["weights"], 16)

        WEIGHTS = 6 * 16
        row_banks = C.banks

        def pe_s():
            pe = nc.tensor
            at = 0
            for n, (W, name, beta, blocks) in enumerate((
                    (WBt, "k0", "l1_b", KT), (WBt, "v0", "l1_b", KT), (WCt, "q0", "l3_b1n", KT), (WCt, "k0", "l3_b1n", KT),
                    (WCt, "v0", "l3_b1n", KT), (WCt, "q1", "l3_b2n", KT), (WCt, "w1", "l3_b3n", MT))):
                yield 20 + 0.5 * n
                pe.wait_ge(setup["weights"], WEIGHTS)
                for m in range(blocks):
                    for k in range(KT):
                        last = mm(B.banks[0][:, at:at + 1], W[name][:, k, m * P:(m + 1) * P], col(beta)[:, k:k + 1],
                                  start=k == 0, stop=k == KT - 1)
                    at += 1
            last.then_inc(setup["fold_ps"], 1)
            for n, (W, name) in enumerate(((WBt, "o0"), (WBt, "o1"), (WCt, "o0"), (WCt, "o1"))):
                yield 41 + 0.5 * n
                pe.wait_ge(setup["spread"], 4)
                pe.wait_ge(setup["scaled"], 9)
                ps = row_banks[n % 2]
                for k in range(KT):
                    last = mm(ps[:, (n // 2) * D:(n // 2 + 1) * D], spread[:, n, k, :], W[name][:, k, :],
                              start=k == 0, stop=k == KT - 1)
                last.then_inc(setup["row_ps"], 1)

        def act_s():
            yield 22
            nc.scalar.wait_ge(setup["weights"], WEIGHTS)
            nc.scalar.activation(tanh_gate[:, :], gate[:, :], ACT.Tanh).then_inc(setup["tanh"], 1)

        def dve_s():
            dve = nc.vector
            yield 22
            dve.wait_ge(setup["weights"], WEIGHTS)
            dve.tensor_scalar(self_add[:, :], self_mul[:, :], 10000.0, -10000.0, ALU.mult, ALU.add).then_inc(setup["step"], 1)
            dve.wait_ge(setup["step"], 1)
            dve.tensor_scalar(self_mul[:, :], self_mul[:, :], HD ** -0.5, None, ALU.mult)
            yield 25
            dve.wait_ge(setup["fold_ps"], 1)
            for name, base in (("bk1", None), ("bv1", None), ("q3", "l3_bqkv"), ("q4", "l3_bq"), ("b1", "l3_b1")):
                at = FOLD[name][0]
                n = 3 * KT if name == "q3" else FOLD[name][1]
                if base:
                    ins = dve.tensor_tensor(fold[:, at:at + n], B.banks[0][:, at:at + n], col(base), ALU.add)
                else:
                    ins = dve.tensor_copy(fold[:, at:at + n], B.banks[0][:, at:at + n])
                ins.then_inc(setup["fold"], 1)
            yield 26
            dve.wait_ge(setup["fold"], 5)
            for n, vec in enumerate((fcol("bv1"), col("l2_bv"), fcol("v3"), col("l3_bv"))):
                dve.tensor_copy(spread[:, n, :, :], bc(vec, 2, P)).then_inc(setup["spread"], 1)
            for n, (W, name, g) in enumerate(((WBt, "k0", "l1_g"), (WBt, "v0", "l1_g"), (WBt, "w1", "l2_post"), (WCt, "q0", "l3_g1"),
                               (WCt, "k0", "l3_g1"), (WCt, "v0", "l3_g1"), (WCt, "q1", "l3_g2"), (WCt, "w1", "l3_g3"))):
                yield 27 + 1.5 * n
                for k in range(KT):
                    last = dve.tensor_scalar(W[name][:, k, :], W[name][:, k, :], col(g)[:, k:k + 1], None, ALU.mult)
                last.then_inc(setup["scaled"], 1)
            yield 39
            dve.wait_ge(setup["tanh"], 1)
            dve.tensor_scalar(WBt["o0"], WBt["o0"], tanh_gate[:, :], None, ALU.mult).then_inc(setup["scaled"], 1)
            yield 46
            dve.wait_ge(setup["row_ps"], 4)
            for at, n, base in ((0, 0, None), (1, 1, "l2_bo"), (3, 2, "l3_bao"), (4, 3, "l3_bco")):
                ps = row_banks[n % 2][:, (n // 2) * D:(n // 2 + 1) * D]
                if base:
                    dve.tensor_tensor(row_bias[:, at, :], ps, rows[:, ROWS.index(base), :], ALU.add)
                else:
                    dve.tensor_copy(row_bias[:, at, :], ps)
            dve.tensor_copy(row_bias[:, 2, :], rows[:, ROWS.index("l2_b2"), :])
            dve.tensor_copy(row_bias[:, 5, :], rows[:, ROWS.index("l3_b2"), :])
        def running(runs, **programs):
            return {name: program() for name, program in programs.items() if name in runs}

        def body(i, a, b, c, load_next=True, store=True):
            first = not b and not c
            runs = "a" * a + "b" * b + "c" * c + "s" * first
            with nc.Block() as block:

                @block.sync
                def _(sp):
                    n = 0
                    if a:
                        sp.dma_start(res_a[:, :], dram["x"][pair(i)].rearrange("n c s -> (n c) s")).then_inc(A["x_in"], 16)
                    if first:
                        load_s(sp)
                    if c and store:
                        sp.dma_start(out[pair(i - 3)].rearrange("n c s -> (n c) s"), y_out[:, :]).then_inc(stored, 16)
                    elif c:
                        sp.sem_inc(stored, 16)
                    if b and a:
                        sp.wait_ge(B.full[0], 1)
                        sp.wait_ge(B.s["xn"], 1)
                        sp.wait_ge(B.s["mask"], 2)
                    if a:
                        n += load_b(sp, i)
                    if c and b:
                        sp.wait_ge(C.full[0], 1)
                        sp.wait_ge(C.s["mask"], 2)
                    if b:
                        n += load_c(sp, i - 1)
                    if a and load_next:
                        sp.wait_ge(A["csplit"], 1)
                        sp.wait_ge(A["norm"], 2)
                        n += load_a(sp, i + 1)
                    if n:
                        sp.wait_ge(loaded, n)
                    if c:
                        sp.wait_ge(stored, 16)

                @block.gpsimd
                def _(pool):
                    weave("pool", running(runs, a=pool_a, b=pool_b, c=pool_c))

                @block.tensor
                def _(pe):
                    weave("pe", running(runs, a=pe_a, b=pe_b, c=pe_c, s=pe_s))

                @block.scalar
                def _(act):
                    weave("act", running(runs, a=act_a, b=act_b, c=act_c, s=act_s))

                @block.vector
                def _(dve):
                    weave("dve", running(runs, a=lambda: dve_a(b), b=lambda: dve_b(c), c=dve_c, s=dve_s))

            nc.all_engine_barrier(sems_to_clear=clear)

        body(0, True, False, False)
        body(1, True, True, False)
        body(2, True, True, True, store=False)
        with nc.Fori(3, PAIRS - 1) as i:
            body(i, True, True, True)
        body(PAIRS - 1, True, True, True, load_next=False)
        body(PAIRS, False, True, True)
        body(PAIRS + 1, False, False, True)
        with nc.Block() as block:

            @block.sync
            def _(sp):
                sp.dma_start(out[pair(PAIRS - 1)].rearrange("n c s -> (n c) s"), y_out[:, :]).then_inc(stored, 16)
                sp.wait_ge(stored, 16)


def _dup(a):
    return np.concatenate([a, a], 0)


def _blocks(a):
    r, n = a.shape
    return np.ascontiguousarray(a.reshape(r // P, P, n).transpose(1, 0, 2).reshape(P, -1))


def kernel(**inputs):
    import concourse.bacc as bacc
    from concourse.bass_utils import run_bass_kernel_spmd

    g = {k: np.asarray(v) for k, v in inputs.items()}
    L0, L1, L2, L3 = ({k.split("_xattn_")[1]: v for k, v in g.items() if k.startswith(f"L{n}_xattn_")} for n in range(4))
    col = lambda v: np.ascontiguousarray(v.reshape(-1, P).T)
    parts = {
        "l0_gamma": _dup(L0["gamma"])[:, None], "l0_beta": _dup(L0["beta"])[:, None], "l0_bo": _dup(L0["bo"])[:, None],
        "l0_bq": _dup(L0["bq"].reshape(H0, S).T), "l0_bk": _dup(L0["bkv"][:H0 * S].reshape(H0, S).T),
        "l1_g": col(L1["ln_gamma"]), "l1_b": col(L1["ln_beta"]),
        "l2_bq": col(L2["q_b"]), "l2_bk": col(L2["kv_b"][0::2]), "l2_bv": col(L2["kv_b"][1::2]),
        "l2_post": col(L2["postnorm_w"]), "l2_b1": col(L2["mlp_b1"]),
        "l3_g1": col(L3["ln1_s"]), "l3_b1n": col(L3["ln1_b"]), "l3_bqkv": col(L3["b_qkv"]),
        "l3_g2": col(L3["ln2_s"]), "l3_b2n": col(L3["ln2_b"]), "l3_bq": col(L3["b_q"]),
        "l3_bk": col(L3["b_kv"][:D]), "l3_bv": col(L3["b_kv"][D:]),
        "l3_g3": col(L3["ln3_s"]), "l3_b3n": col(L3["ln3_b"]), "l3_b1": col(L3["b1"]),
    }
    wide = lambda w: np.stack([w, w], 2).reshape(w.shape[0], H0 * P)
    heads_T = lambda w: w.T.reshape(S, H0, S)
    wqkv, wkv3 = L3["w_qkv"], L3["w_kv"]
    arrays = {
        "x": g["x"], "ctx": g["ctx_2048"],
        "mask1": g["mask_BxS2_bf1"].view(np.uint8), "mask2": g["mask_BxS2_ik0"],
        "self_mask": g["mask_1x1xSxS2_fc1"].reshape(S, S), "mask4": g["mask_Bx1xSxS2_ff1"].reshape(NSEQ, S, S),
        "cols": np.concatenate([parts[n] for n in COLS], 1),
        "rows": np.stack([L2["out_b"], L2["mlp_b2"], L3["b_ao"], L3["b_co"], L3["b2"]]),
        "gate": L1["gate"],
        "wq0": _dup(wide(heads_T(L0["Wq"]))), "wk0": _dup(wide(heads_T(L0["Wkv"][:H0 * S]))),
        "wv0": wide(L0["Wkv"][H0 * S:].reshape(H0, S, S).transpose(1, 0, 2)),
        "wo0": np.ascontiguousarray(L0["Wo"].reshape(S, H0, S).transpose(2, 1, 0)).reshape(S, H0 * S),
        "bv0": np.ascontiguousarray(L0["bkv"][H0 * S:].reshape(H0, S).T),
        "wb": np.concatenate([_blocks(w) for w in (L1["Wq"].T, L1["Wk"].T, L1["Wv"].T, L1["Wo"].T, L2["q_w"], L2["kv_w"][:, 0::2],
                                                   L2["kv_w"][:, 1::2], L2["out_w"], L2["mlp_w1"], L2["mlp_w2"])], 1),
        "wc": np.concatenate([_blocks(w) for w in (wqkv[:, :D], wqkv[:, D:2 * D], wqkv[:, 2 * D:], L3["w_ao"], L3["w_q"], wkv3[:, :D],
                                                   wkv3[:, D:], L3["w_co"], L3["w1"], L3["w2"])], 1),
    }
    arrays = {f"in_{n}": np.ascontiguousarray(a) for n, a in arrays.items()}
    nc = bacc.Bacc("TRN2", target_bir_lowering=False, num_devices=1)
    dram = {n[3:]: nc.dram_tensor(n, a.shape, mybir.dt.from_np(a.dtype), kind="ExternalInput").ap() for n, a in arrays.items()}
    out = nc.dram_tensor("out", (NSEQ, S, D), F32, kind="ExternalOutput").ap()
    build(nc, dram, out)
    got = run_bass_kernel_spmd(nc, [arrays], core_ids=[0])
    return got.results[0]["out"]
```
